# Optimizing a Trainium2 kernel written in Bass

```python
import numpy as np
import jax
import jax.numpy as jnp

def _softmax(x, axis=-1):
    return jax.nn.softmax(x, axis=axis)

def _gelu(x):
    return jax.nn.gelu(x, approximate=True)

def _silu(x):
    return jax.nn.silu(x)

def _sigmoid(x):
    return jax.nn.sigmoid(x)

def _layernorm(x, axis=-1, eps=1e-05):
    m = jnp.mean(x, axis=axis, keepdims=True)
    v = jnp.var(x, axis=axis, keepdims=True)
    return (x - m) / jnp.sqrt(v + eps)

def _scatter_add(tgt, idx, src, axis=0):
    return tgt.at[idx].add(src)

def _segment_sum(src, seg, n):
    return jax.ops.segment_sum(src, seg, n)
kernel_name = 'mk_cond_seq_d2_seqx_r4_262794'

def setup_inputs(seed: int=0):
    np.random.seed(seed)
    _w = jnp.asarray

    def _rec_inputs():
        import jax
        import jax.numpy as jnp
        _rk = jax.random.key(seed)
        x = -7.109e-05 + 0.9999 * jax.random.normal(jax.random.fold_in(_rk, 1), (4, 512, 256), jnp.float32)
        _lenS = 512 - jax.random.randint(jax.random.fold_in(_rk, 7), (4,), 0, max(1, 512 // 4) + 1, jnp.int32)
        _lenS2 = 512 - jax.random.randint(jax.random.fold_in(_rk, 8), (4,), 0, max(1, 512 // 4) + 1, jnp.int32)
        condB_theta = jax.random.uniform(jax.random.fold_in(_rk, 11), (4,), jnp.float32, 0.0, 0.983423)
        condB_phi = jax.random.uniform(jax.random.fold_in(_rk, 12), (4,), jnp.float32, 0.0, 0.961312)
        itok_B_34_63 = jax.random.randint(jax.random.fold_in(_rk, 14), (4,), 34, 64, jnp.int32)
        fside_Bx16xSxS_0 = -1.47943e-05 + 1.00017 * jax.random.normal(jax.random.fold_in(_rk, 15), (4, 16, 512, 512), jnp.float32)
        _validS = jnp.arange(512)[None, :] < _lenS[:, None]
        _validS2 = jnp.arange(512)[None, :] < _lenS2[:, None]
        _causal = jnp.tril(jnp.ones((512, 512), dtype=bool))
        mask_Bx1xSxS_bk0 = jnp.logical_not(jnp.broadcast_to(_validS[:, None, None, :], (4, 1, 512, 512)))
        return (x, condB_theta, condB_phi, itok_B_34_63, fside_Bx16xSxS_0, mask_Bx1xSxS_bk0)
    x, condB_theta, condB_phi, itok_B_34_63, fside_Bx16xSxS_0, mask_Bx1xSxS_bk0 = _rec_inputs()

    def _L0_cond_setup():
        import jax, jax.numpy as jnp
        import numpy as np
        key = jax.random.key(seed)
        k1, k2, k3 = jax.random.split(key, 3)
        B, N, D = (16, 1024, 256)
        embeddings = jax.random.normal(k1, (B, N, D), dtype=jnp.float32)
        theta = jax.random.uniform(k2, (B,), dtype=jnp.float32)
        phi = jax.random.uniform(k3, (B,), dtype=jnp.float32)
        return {'embeddings': embeddings, 'theta': theta, 'phi': phi}
    _L0_cond_all = _L0_cond_setup()
    _L0_cond_in = {k: v for k, v in _L0_cond_all.items() if k in ()}
    del _L0_cond_all

    def _L1_cond_setup():
        import jax, jax.numpy as jnp
        import numpy as np
        import math
        D_MODEL = 256
        N_HEAD = 16
        HEAD_DIM = D_MODEL // N_HEAD
        D_FF = 1024
        NUM_STEPS = 100.0
        RESCALE = 4000.0
        EPS = 1e-05

        def _sin_emb(t):
            half = D_MODEL // 2
            x = t.astype(jnp.float32) / NUM_STEPS * RESCALE
            freqs = jnp.exp(jnp.arange(half, dtype=jnp.float32) * (-math.log(10000.0) / (half - 1)))
            e = x[:, None] * freqs[None, :]
            return jnp.concatenate([jnp.sin(e), jnp.cos(e)], axis=-1)

        def _ln(x):
            m = jnp.mean(x, axis=-1, keepdims=True)
            v = jnp.var(x, axis=-1, keepdims=True)
            return (x - m) / jnp.sqrt(v + EPS)

        def _gelu2(x):
            return x * jax.nn.sigmoid(1.702 * x)
        key = jax.random.key(seed)
        ks = jax.random.split(key, 24)
        B, S, D, F = (4, 128, D_MODEL, D_FF)
        std = 0.02
        inp = {'src': jax.random.normal(ks[0], (B, S, D), dtype=jnp.float32), 'src_mask': jax.random.randint(ks[1], (B, 1, S, S), 0, 2).astype(bool), 'timestep': jax.random.randint(ks[2], (B,), 0, 100, dtype=jnp.int32), 'attention_bias': jax.random.normal(ks[3], (B, N_HEAD, S, S), dtype=jnp.float32), 'W_ada': jax.random.normal(ks[4], (D, 2 * D), dtype=jnp.float32) * std, 'b_ada': jnp.zeros((2 * D,), dtype=jnp.float32), 'Wq': jax.random.normal(ks[5], (D, D), dtype=jnp.float32) * std, 'bq': jnp.zeros((D,), dtype=jnp.float32), 'Wk': jax.random.normal(ks[6], (D, D), dtype=jnp.float32) * std, 'bk': jnp.zeros((D,), dtype=jnp.float32), 'Wv': jax.random.normal(ks[7], (D, D), dtype=jnp.float32) * std, 'bv': jnp.zeros((D,), dtype=jnp.float32), 'Wo': jax.random.normal(ks[8], (D, D), dtype=jnp.float32) * std, 'bo': jnp.zeros((D,), dtype=jnp.float32), 'W1': jax.random.normal(ks[9], (D, F), dtype=jnp.float32) * std, 'b1': jnp.zeros((F,), dtype=jnp.float32), 'W2': jax.random.normal(ks[10], (F, D), dtype=jnp.float32) * std, 'b2': jnp.zeros((D,), dtype=jnp.float32), 'g2': jnp.ones((D,), dtype=jnp.float32), 'beta2': jnp.zeros((D,), dtype=jnp.float32)}
        return inp
    _L1_cond_all = _L1_cond_setup()
    _L1_cond_in = {k: v for k, v in _L1_cond_all.items() if k in ('W_ada', 'b_ada', 'Wq', 'bq', 'Wk', 'bk', 'Wv', 'bv', 'Wo', 'bo', 'W1', 'b1', 'W2', 'b2', 'g2', 'beta2')}
    del _L1_cond_all
    return {'x': x, 'condB_theta': condB_theta, 'condB_phi': condB_phi, 'itok_B_34_63': itok_B_34_63, 'fside_Bx16xSxS_0': fside_Bx16xSxS_0, 'mask_Bx1xSxS_bk0': mask_Bx1xSxS_bk0, 'L1_cond_W_ada': _L1_cond_in['W_ada'], 'L1_cond_b_ada': _L1_cond_in['b_ada'], 'L1_cond_Wq': _L1_cond_in['Wq'], 'L1_cond_bq': _L1_cond_in['bq'], 'L1_cond_Wk': _L1_cond_in['Wk'], 'L1_cond_bk': _L1_cond_in['bk'], 'L1_cond_Wv': _L1_cond_in['Wv'], 'L1_cond_bv': _L1_cond_in['bv'], 'L1_cond_Wo': _L1_cond_in['Wo'], 'L1_cond_bo': _L1_cond_in['bo'], 'L1_cond_W1': _L1_cond_in['W1'], 'L1_cond_b1': _L1_cond_in['b1'], 'L1_cond_W2': _L1_cond_in['W2'], 'L1_cond_b2': _L1_cond_in['b2'], 'L1_cond_g2': _L1_cond_in['g2'], 'L1_cond_beta2': _L1_cond_in['beta2']}

def reference(x, condB_theta, condB_phi, itok_B_34_63, fside_Bx16xSxS_0, mask_Bx1xSxS_bk0, L1_cond_W_ada, L1_cond_b_ada, L1_cond_Wq, L1_cond_bq, L1_cond_Wk, L1_cond_bk, L1_cond_Wv, L1_cond_bv, L1_cond_Wo, L1_cond_bo, L1_cond_W1, L1_cond_b1, L1_cond_W2, L1_cond_b2, L1_cond_g2, L1_cond_beta2):
    import jax
    import jax.numpy as jnp

    def _L0_cond_ref(embeddings, theta, phi):
        import jax, jax.numpy as jnp
        import numpy as np
        B, N, D = embeddings.shape
        e = embeddings.reshape(B, N, D // 4, 4)
        ct = jnp.cos(theta)[:, None, None]
        st = jnp.sin(theta)[:, None, None]
        cp = jnp.cos(phi)[:, None, None]
        sp = jnp.sin(phi)[:, None, None]
        x0, x1, x2, x3 = (e[..., 0], e[..., 1], e[..., 2], e[..., 3])
        out = jnp.stack([x0 * ct + x1 * st, -x0 * st + x1 * ct, x2 * cp + x3 * sp, -x2 * sp + x3 * cp], axis=-1)
        return out.reshape(B, N, D)

    def _L1_cond_ref(src, src_mask, timestep, attention_bias, W_ada, b_ada, Wq, bq, Wk, bk, Wv, bv, Wo, bo, W1, b1, W2, b2, g2, beta2):
        import jax, jax.numpy as jnp
        import numpy as np
        import math
        D_MODEL = 256
        N_HEAD = 16
        HEAD_DIM = D_MODEL // N_HEAD
        D_FF = 1024
        NUM_STEPS = 100.0
        RESCALE = 4000.0
        EPS = 1e-05

        def _sin_emb(t):
            half = D_MODEL // 2
            x = t.astype(jnp.float32) / NUM_STEPS * RESCALE
            freqs = jnp.exp(jnp.arange(half, dtype=jnp.float32) * (-math.log(10000.0) / (half - 1)))
            e = x[:, None] * freqs[None, :]
            return jnp.concatenate([jnp.sin(e), jnp.cos(e)], axis=-1)

        def _ln(x):
            m = jnp.mean(x, axis=-1, keepdims=True)
            v = jnp.var(x, axis=-1, keepdims=True)
            return (x - m) / jnp.sqrt(v + EPS)

        def _gelu2(x):
            return x * jax.nn.sigmoid(1.702 * x)
        B, S, D = src.shape
        emb = jax.nn.silu(_sin_emb(timestep)) @ W_ada + b_ada
        scale, shift = jnp.split(emb[:, None, :], 2, axis=-1)
        x = _ln(src) * (1.0 + scale) + shift
        q = (x @ Wq + bq).reshape(B, S, N_HEAD, HEAD_DIM).transpose(0, 2, 1, 3)
        k = (x @ Wk + bk).reshape(B, S, N_HEAD, HEAD_DIM).transpose(0, 2, 1, 3)
        v = (x @ Wv + bv).reshape(B, S, N_HEAD, HEAD_DIM).transpose(0, 2, 1, 3)
        scores = jnp.einsum('bhqd,bhkd->bhqk', q / math.sqrt(HEAD_DIM), k)
        scores = scores + attention_bias
        scores = jnp.where(src_mask, -jnp.inf, scores.astype(jnp.float32))
        probs = jax.nn.softmax(scores, axis=-1).astype(v.dtype)
        ctx = jnp.einsum('bhqk,bhkd->bhqd', probs, v)
        ctx = ctx.transpose(0, 2, 1, 3).reshape(B, S, D)
        x = x + (ctx @ Wo + bo)
        h = _ln(x) * g2 + beta2
        ff = _gelu2(h @ W1 + b1) @ W2 + b2
        return x + ff
    x = _L0_cond_ref(x, condB_theta, condB_phi)
    x = _L1_cond_ref(x, mask_Bx1xSxS_bk0, itok_B_34_63, fside_Bx16xSxS_0, L1_cond_W_ada, L1_cond_b_ada, L1_cond_Wq, L1_cond_bq, L1_cond_Wk, L1_cond_bk, L1_cond_Wv, L1_cond_bv, L1_cond_Wo, L1_cond_bo, L1_cond_W1, L1_cond_b1, L1_cond_W2, L1_cond_b2, L1_cond_g2, L1_cond_beta2)
    return x

_drawn_inputs = setup_inputs


def setup_inputs(seed=0):
    import zlib

    import numpy as np

    out = dict(_drawn_inputs(seed))
    spreads = {'L1_cond_b_ada': (0.0, 0.1),
     'L1_cond_bq': (0.0, 0.8),
     'L1_cond_bk': (0.0, 2.0),
     'L1_cond_bv': (0.0, 0.275),
     'L1_cond_bo': (0.0, 0.1),
     'L1_cond_b1': (0.0, 0.1),
     'L1_cond_b2': (0.0, 0.1),
     'L1_cond_g2': (1.0, 0.6),
     'L1_cond_beta2': (0.0, 0.673)}
    factors = {'fside_Bx16xSxS_0': 8.0, 'L1_cond_Wq': 8.0, 'L1_cond_Wk': 8.0, 'L1_cond_Wv': 3.139}
    for name, (base, spread) in spreads.items():
        noise = np.random.default_rng([zlib.crc32(name.encode()), seed]).standard_normal(out[name].shape)
        drawn = base * np.exp(spread * noise) if base else spread * noise
        out[name] = jnp.asarray(drawn.astype(out[name].dtype))
    for name, factor in factors.items():
        out[name] = (out[name] * factor).astype(out[name].dtype)
    return out
```

```python
from contextlib import ExitStack
import math

import numpy as np

import concourse.bass as bass
from concourse import mybir

F32 = mybir.dt.float32
BF16 = mybir.dt.bfloat16
I32 = mybir.dt.int32
U8 = mybir.dt.uint8
U32 = mybir.dt.uint32
ALU = mybir.AluOpType
ACT = mybir.ActivationFunctionType

B, S, D, H, DH, F = 4, 512, 256, 16, 16, 1024
P = 128
NT = S // P
TILES = B * NT
NC = D // P
NF = F // P
QUADS = H // 4
HALF = 2 * P
HALVES = 2 * QUADS
UNITS = 8 * HALVES
LOADS = UNITS // 4
RING = 4
NSC = 4
VW = 32
ONE = DH

EPS = 1e-5
MASKED = -1e30
LOWEST = -3.0e38
INV_2PI = 1.0 / (2.0 * math.pi)
ROUND = 12582912.0
TWO_PI_A = 6.28125
TWO_PI_B = float(np.float32(np.round((2.0 * math.pi - TWO_PI_A) * 2**22) / 2**22))
TWO_PI_C = 2.0 * math.pi - TWO_PI_A - TWO_PI_B
PI_IN = 3.1415925

TERMS = [(0, 0), (0, 1), (1, 0), (1, 1), (0, 2), (2, 0)]
ROWS = len(TERMS) * DH
MOVES = 2 * len(TERMS)

SIN_E, COS_E, COS_T, SIN_T, COS_P, SIN_P, ANGLES = 0, 4, 8, 12, 16, 20, 24
C_ID, C_FREQ, C_TURN, C_PHASE, C_ALL = 0, P, P + 1, P + 1 + 24, P + 1 + 48

SLICE_AT = [36, 40, 44, 48]


def constants():
    c = np.zeros((P, C_ALL), np.float32)
    c[:, C_ID:C_ID + P] = np.eye(P, dtype=np.float32)
    step = np.float32(-math.log(10000.0) / (P - 1))
    c[:, C_FREQ] = np.exp(np.arange(P, dtype=np.float32) * step)
    for at in (COS_E, COS_T, COS_P):
        c[:, C_TURN + at:C_TURN + at + 4] = 0.25
        c[:, C_PHASE + at:C_PHASE + at + 4] = math.pi / 2
    return c


def rotate_then_attend_then_feed_forward(nc, x, theta, phi, timestep, bias, mask, w_ada, b_ada, wq, bq, wk, bk,
                                         wv, bv, wo, bo, w1, b1, w2, b2, g2, beta2, const, out):
    ctx = ExitStack()
    with ctx:
        def sb(name, shape, dt=F32):
            return ctx.enter_context(nc.sbuf_tensor(name, shape, dt))

        def sem(name):
            return ctx.enter_context(nc.semaphore(name))

        part_rows = nc.dram_tensor("part_rows", (3, 4, P, S), BF16, kind="Internal").ap()

        bank_s = [ctx.enter_context(nc.psum_tensor(f"bank_s{i}", [P, S], F32)) for i in range(2)]
        bank_t = [ctx.enter_context(nc.psum_tensor(f"bank_t{i}", [P, S], F32)) for i in range(2)]
        bank_c = [ctx.enter_context(nc.psum_tensor(f"bank_c{i}", [P, S], F32)) for i in range(2)]
        bank_m = [ctx.enter_context(nc.psum_tensor(f"bank_m{i}", [P, S], F32)) for i in range(2)]

        ring = sb("ring", [P, RING, 2, 2, S])
        probs = sb("probs", [P, 2, 4, NT, HALF])
        scores = sb("scores", [P, NSC, S])
        stack_q = sb("stack_q", [ROWS, 2, 4, S], BF16)
        stack_k = sb("stack_k", [ROWS, 2, 4, S], BF16)
        parts = sb("parts", [P, 3, 4, S], BF16)
        qk_full = sb("qk_full", [P, 4, P])
        qk_rest = sb("qk_rest", [P, 4, P])
        x_now = sb("x_now", [P, D])
        xT = sb("xT", [P, NC, P])
        X = sb("X", [P, TILES, D])
        V = sb("V", [P, NT, H, VW])
        V_next = sb("V_next", [P, NT, H, VW])
        mask_add = sb("mask_add", [P, TILES, S], BF16)
        ctx_raw = sb("ctx_raw", [P, 2, HALF])
        ctx_sum = sb("ctx_sum", [P, 2, 4])
        ctx_tok = sb("ctx_tok", [P, NT, D])
        ctxT = sb("ctxT", [P, NC, S])
        cst = sb("cst", [P, C_ALL])
        w_qk = sb("w_qk", [P, NC, 2 * D])
        w_v = sb("w_v", [P, NC, D])
        w_o = sb("w_o", [P, NC, D])
        b_qk = sb("b_qk", [P, 4])
        bv_row = sb("bv_row", [P, D])
        bo_row = sb("bo_row", [P, D])
        b2_row = sb("b2_row", [P, D])
        b1_col = sb("b1_col", [P, NF])
        g2_col = sb("g2_col", [P, NC])
        beta2_col = sb("beta2_col", [P, NC])
        eps = sb("eps", [P, 1])
        pool_spare = sb("pool_spare", [P, RING])
        dve_spare = sb("dve_spare", [P, 2])
        t_int = sb("t_int", [P, B], I32)
        angle = sb("angle", [P, ANGLES])
        turns = sb("turns", [P, ANGLES])
        sincos = sb("sincos", [P, ANGLES])
        minus = sb("minus", [P, ANGLES])
        emb = sb("emb", [P, 8])
        stats = sb("stats", [P, TILES, 6])
        meanvar = sb("meanvar", [P, TILES, 2])
        stats2 = sb("stats2", [P, TILES, 6])
        meanvar2 = sb("meanvar2", [P, TILES, 2])
        sd = sb("sd", [P, TILES])
        rstd = sb("rstd", [P, TILES])
        sd2 = sb("sd2", [P, TILES])
        rstd2 = sb("rstd2", [P, TILES])
        row_max = sb("row_max", [P, NSC])
        ident = cst[:, C_ID:C_ID + P]

        flat = probs[:, :, :, :, :].rearrange("p a h k q -> p (a h k q)")
        x_raw = flat[:, 0:TILES * D].rearrange("p (t d) -> p t d", t=TILES)
        mask_words = flat[:, TILES * D:TILES * D + TILES * S // 4].bitcast(U32)
        mask_raw = mask_words.bitcast(U8).rearrange("p (t k) -> p t k", t=TILES)
        row_scale = scores[:, :, :]
        wide = V[:, :, :, :].rearrange("p a h w -> p (a h w)")
        emb_wide = wide[:, 0:8 * P].rearrange("p (c n) -> p c n", c=8)
        vn = V_next[:, :, :, :].rearrange("p a h w -> p (a h w)")
        w_ada_sb = ctxT[:, :, :]
        b_ada_row = ctx_raw[:, :, :].rearrange("p a n -> p (a n)")
        rflat = ring[:, :, :, :, :].rearrange("p r h t k -> p (r h t k)")
        w1_sb = rflat[:, 0:NC * F].rearrange("p (c f) -> p c f", c=NC)
        w2_sb = rflat[:, NC * F:NC * F + NF * D].rearrange("p (c d) -> p c d", c=NF)
        gT = rflat[:, 4096:8192].rearrange("p (c n) -> p c n", c=NF)
        h_now = flat[:, 0:1024].rearrange("p (t d) -> p t d", t=NT)
        hT = flat[:, 1024:2048].rearrange("p (c n) -> p c n", c=NC)
        yb = flat[:, 2048:3072].rearrange("p (t d) -> p t d", t=NT)
        o_sb = flat[:, 4096:6144].rearrange("p (a t d) -> p a t d", a=2, t=NT)

        angles_in = sem("angles_in")
        x_in = [sem(f"x_in{b}") for b in range(B)]
        mask_in = sem("mask_in")
        ada_in = sem("ada_in")
        proj_in = sem("proj_in")
        rows_in = sem("rows_in")
        ffn_in = sem("ffn_in")
        bias_in = [sem(f"bias_in{i}") for i in range(RING)]
        stored = sem("stored")
        stacked = [sem(f"stacked{i}") for i in range(2)]
        out_in = [sem(f"out_in{i}") for i in range(2)]
        ready = sem("ready")
        angle_step = sem("angle_step")
        sin_done = sem("sin_done")
        silu_done = sem("silu_done")
        wide_done = sem("wide_done")
        emb_done = sem("emb_done")
        row_done = sem("row_done")
        minus_done = sem("minus_done")
        cos_part = sem("cos_part")
        rotated = sem("rotated")
        stat_done = sem("stat_done")
        aggr_done = sem("aggr_done")
        sd_done = sem("sd_done")
        rstd_done = sem("rstd_done")
        centred = sem("centred")
        normed = sem("normed")
        mask_done = sem("mask_done")
        wscaled = sem("wscaled")
        x_copied = sem("x_copied")
        x_turned = sem("x_turned")
        xT_out = sem("xT_out")
        qk_proj = sem("qk_proj")
        qk_out = sem("qk_out")
        v_proj = sem("v_proj")
        v_out = sem("v_out")
        cast1 = sem("cast1")
        rest1 = sem("rest1")
        cast2 = sem("cast2")
        rest2 = sem("rest2")
        v_moved = sem("v_moved")
        masked = sem("masked")
        qk_done = sem("qk_done")
        summed = sem("summed")
        shifted = sem("shifted")
        turned = sem("turned")
        exped = sem("exped")
        pv_done = sem("pv_done")
        ctx_out = sem("ctx_out")
        ctx_turned = sem("ctx_turned")
        ctx_recip = sem("ctx_recip")
        ctx_norm = sem("ctx_norm")
        back_turned = sem("back_turned")
        back_out = sem("back_out")
        wo_done = sem("wo_done")
        wo_bias = sem("wo_bias")
        y_done = sem("y_done")
        h_done = sem("h_done")
        h_turned = sem("h_turned")
        hT_out = sem("hT_out")
        ff1_done = sem("ff1_done")
        gelu_done = sem("gelu_done")
        ff2_done = sem("ff2_done")
        yb_done = sem("yb_done")
        o_done = sem("o_done")

        FREE_S, FREE_SC, FREE_T, FREE_P, FREE_C, FREE_R, FREE_G, FREE_1 = 2, NSC, 2, 2, 2, 2, 4, 1

        def unit(u):
            blk, j, q = u // 8, u % 8 // 2, u % 2
            return blk, j, 2 * (blk % 2) + q

        def ff_bank(f):
            return (bank_t + bank_c)[f % 4]

        block = ctx.enter_context(nc.Block())

        @block.sync
        def _(sp):
            sp.dma_start(cst[:, :], const).then_inc(angles_in, 16)
            for src, at in ((timestep, None), (theta, COS_T), (theta, SIN_T), (phi, COS_P), (phi, SIN_P)):
                dst = t_int[:, :] if at is None else angle[:, at:at + B]
                sp.dma_start(dst, src.rearrange("(o b) -> o b", o=1).broadcast_to([P, B])).then_inc(angles_in, 16)
            sp.dma_start(w_ada_sb, w_ada.rearrange("(c p) n -> p c n", p=P)).then_inc(ada_in, 16)
            sp.dma_start(b_ada_row, b_ada.rearrange("(o n) -> o n", o=1).broadcast_to([P, 2 * D])).then_inc(ada_in, 16)
            for b in range(B):
                sp.dma_start(x_raw[:, NT * b:NT * b + NT, :], x[b].rearrange("(t p) d -> p t d", p=P)).then_inc(x_in[b], 16)
            for w, at in ((wq, 0), (wk, D)):
                sp.dma_start(w_qk[:, :, at:at + D], w.rearrange("(c p) n -> p c n", p=P)).then_inc(proj_in, 16)
            sp.dma_start(w_v[:, :, :], wv.rearrange("(c p) n -> p c n", p=P)).then_inc(proj_in, 16)
            sp.dma_start(w_o[:, :, :], wo.rearrange("(c p) n -> p c n", p=P)).then_inc(proj_in, 16)
            for v, at in ((bq, 0), (bk, 2)):
                sp.dma_start(b_qk[:, at:at + 2], v).then_inc(proj_in, 16)
            sp.dma_start(mask_words.rearrange("p (t k) -> p t k", t=TILES), mask.rearrange("b o (t p) k -> p (b o t) k", p=P)).then_inc(mask_in, 16)
            for v, row in ((bv, bv_row), (bo, bo_row), (b2, b2_row)):
                sp.dma_start(row[:, :], v.rearrange("(o n) -> o n", o=1).broadcast_to([P, D])).then_inc(rows_in, 16)
            sp.dma_start(b1_col[:, :], b1).then_inc(rows_in, 16)
            sp.dma_start(g2_col[:, :], g2).then_inc(rows_in, 16)
            sp.dma_start(beta2_col[:, :], beta2).then_inc(rows_in, 16)

            def load_bias(b, c, first=False):
                if not first:
                    sp.wait_ge(summed, b * UNITS + 4 * (c - RING) + 4 + FREE_S)
                blk, h = c // 2, 4 * (c // 4) + 2 * (c % 2)
                q0 = HALF * (blk % 2)
                src = bias[b] if first else bias[bass.ds(b, 1)].rearrange("o h q k -> (o h) q k")
                for i in range(2):
                    sp.dma_start(ring[:, c % RING, i, :, :], src[h + i, q0:q0 + HALF, :].rearrange("(t p) k -> p t k", p=P))\
                        .then_inc(bias_in[c % RING], 16)

            def await_all(*pairs):
                pairs = [(s, n if isinstance(n, int) else sp.snap(n)) for s, n in pairs]
                for s, n in pairs:
                    sp.wait_ge(s, n)

            def store_parts(b):
                split = NT * (b + 1)
                before = [] if isinstance(b, int) and b == 0 else [(stacked[i], b * (2 * MOVES * 16)) for i in range(2)]
                await_all((rest2, split), (cast2, split), *before)
                for i in range(3):
                    sp.dma_start(part_rows[i].rearrange("m p n -> p m n"), parts[:, i, :, :]).then_inc(stored, 16)

            def stack(b, g, first=False):
                if not first:
                    sp.wait_ge(qk_done, b * UNITS + 16 * (g - 1))
                if g == 0:
                    sp.wait_ge(stored, b * 48 + 48)
                r = 64 * (g % 2)
                for t, pair in enumerate(TERMS):
                    for dst, part, m in ((stack_q, pair[0], g // 2), (stack_k, pair[1], 2 + g // 2)):
                        sp.dma_start(dst[DH * t:DH * t + DH, g % 2, :, :],
                                     part_rows[part, m, r:r + 64, :].rearrange("(h d) n -> d h n", h=4))\
                            .then_inc(stacked[g % 2], 16)

            for c in range(RING):
                load_bias(0, c, first=True)
            store_parts(0)
            stack(0, 0, first=True)
            stack(0, 1, first=True)

            def batch(b, last):
                for c in range(RING, LOADS + RING):
                    if c < LOADS:
                        load_bias(b, c)
                    elif not last:
                        load_bias(b + 1, c - LOADS)
                    if c == 6:
                        stack(b, 2)
                    if c == 10:
                        stack(b, 3)
                    if c == 14 and not last:
                        store_parts(b + 1)
                    if c == 15 and not last:
                        stack(b + 1, 0)
                if not last:
                    stack(b + 1, 1)

            with sp.Fori(0, B - 1) as b:
                batch(b, False)
            batch(B - 1, True)

            sp.wait_ge(summed, B * UNITS + FREE_S)
            sp.dma_start(w1_sb, w1.rearrange("(c p) f -> p c f", p=P)).then_inc(ffn_in, 16)
            sp.dma_start(w2_sb, w2.rearrange("(c p) d -> p c d", p=P)).then_inc(ffn_in, 16)
            for b in range(B):
                for t in range(NT):
                    sp.wait_ge(o_done, NT * b + t + 1 + FREE_1)
                    sp.dma_start(out[b, P * t:P * t + P, :], o_sb[:, b % 2, t, :]).then_inc(out_in[b % 2], 16)
            for i in range(2):
                sp.wait_ge(out_in[i], 16 * TILES // 2)

        @block.gpsimd
        def _(pool):
            pool.memset(eps[:, :], EPS).then_inc(ready, 1)
            pool.memset(V_next[:, :, :, :], 0.0).then_inc(ready, 1)
            pool.wait_ge(ready, 2)
            pool.memset(V_next[:, :, :, ONE:ONE + 1], 1.0).then_inc(ready, 1)

            def mask_bias(b, c, h):
                if h == 0:
                    pool.wait_ge(bias_in[c % RING], (b * (LOADS // RING) + c // RING + 1) * 32)
                    pool.tensor_tensor(pool_spare[:, c % RING:c % RING + 1], eps[:, :], eps[:, :], ALU.add)
                q = 2 * (c // 2 % 2)
                src = ring[:, c % RING, h, :, :]
                pool.tensor_tensor(src, src, mask_add[:, bass.ds(b * NT + q, 2), :], ALU.add).then_inc(masked, 1)

            def first_rest(s, t):
                pool.wait_ge(qk_out, s + 1)
                pool.wait_ge(cast1, s + 1)
                pool.wait_ge(cast2, s)
                pool.wait_ge(rest2, s)
                pool.tensor_tensor(qk_rest[:, :, :], qk_full[:, :, :], parts[:, 0, :, P * t:P * t + P], ALU.subtract)\
                    .then_inc(rest1, 1)

            def second_rest(s, t):
                pool.wait_ge(rest1, s + 1)
                pool.wait_ge(cast2, s + 1)
                pool.tensor_tensor(parts[:, 2, :, P * t:P * t + P], qk_rest[:, :, :], parts[:, 1, :, P * t:P * t + P],
                                   ALU.subtract).then_inc(rest2, 1)

            pool.wait_ge(mask_done, 1)
            for c in range(2):
                mask_bias(0, c, 0)
                mask_bias(0, c, 1)
            for t in range(NT):
                first_rest(t, t)
                second_rest(t, t)

            def batch(b, last):
                for c in range(2, LOADS + 2):
                    for h in range(2):
                        if c < LOADS:
                            mask_bias(b, c, h)
                        elif not last:
                            mask_bias(b + 1, c - LOADS, h)
                        t = c - (SLICE_AT[0] // 4 + 2)
                        if 0 <= t < NT and not last:
                            if h == 0:
                                first_rest((b + 1) * NT + t, t)
                            else:
                                second_rest((b + 1) * NT + t, t)

            with pool.Fori(0, B - 1) as b:
                batch(b, False)
            batch(B - 1, True)

            pool.wait_ge(rows_in, 16 * 6)
            with pool.Fori(0, B) as b:
                pool.wait_ge(y_done, B * 2 + FREE_1)
                pool.wait_ge(o_done, b * NT + FREE_1)
                pool.tensor_tensor(yb, X[:, bass.ds(b * NT, NT), :],
                                   b2_row[:, :].rearrange("p (o d) -> p o d", o=1).broadcast_to([P, NT, D]),
                                   ALU.add).then_inc(yb_done, 1)

        @block.scalar
        def _(act):
            act.wait_ge(angle_step, 10)
            act.activation(sincos[:, :], angle[:, :], ACT.Sin).then_inc(sin_done, 1)
            act.wait_ge(sin_done, 1)
            act.activation(emb[:, :], sincos[:, SIN_E:COS_E + B], ACT.Silu).then_inc(silu_done, 1)
            for b in range(B):
                act.wait_ge(x_in[b], 16)
                for pair, at in ((0, COS_T), (2, COS_P)):
                    src, dst = (v[:, NT * b:NT * b + NT, :].rearrange("p t (n e) -> p (t n) e", e=4)[:, :, pair:pair + 2]
                                for v in (x_raw, X))
                    act.activation(dst, src, ACT.Copy, scale=sincos[:, at + b:at + b + 1]).then_inc(cos_part, 1)
            act.wait_ge(mask_in, 16)
            act.activation(mask_add[:, 0:NT, :], mask_raw[:, 0:NT, :], ACT.Copy, scale=MASKED)
            act.activation(mask_add[:, NT:TILES, :], mask_raw[:, NT:TILES, :], ACT.Copy, scale=MASKED).then_inc(mask_done, 1)
            act.wait_ge(aggr_done, TILES)
            act.wait_ge(ready, 1)
            act.activation(sd[:, :], meanvar[:, :, 1], ACT.Sqrt, bias=eps[:, 0:1]).then_inc(sd_done, 1)
            act.wait_ge(proj_in, 16 * 6)
            act.activation(w_qk[:, :, 0:D], w_qk[:, :, 0:D], ACT.Copy, scale=DH ** -0.5).then_inc(wscaled, 1)
            act.activation(b_qk[:, 0:2], b_qk[:, 0:2], ACT.Copy, scale=DH ** -0.5).then_inc(wscaled, 1)

            def copy_x(s):
                act.wait_ge(x_turned, s)
                src = X[:, bass.ds(s, 1), :].rearrange("p o d -> p (o d)")
                act.activation(x_now[:, :], src, ACT.Copy).then_inc(x_copied, 1)

            def copy_xT(s):
                act.wait_ge(x_turned, s + 1)
                act.wait_ge(v_proj, s)
                act.activation(xT[:, :, :], bank_m[1][:, 0:NC * P].rearrange("p (c n) -> p c n", c=NC), ACT.Copy)\
                    .then_inc(xT_out, 1)

            def cast_first(s, t, b, first=False):
                act.wait_ge(qk_out, s + 1)
                if t == 0 and not first:
                    act.wait_ge(stored, b * 48)
                act.activation(parts[:, 0, :, P * t:P * t + P], qk_full[:, :, :], ACT.Copy).then_inc(cast1, 1)

            def cast_second(s, t):
                act.wait_ge(rest1, s + 1)
                act.activation(parts[:, 1, :, P * t:P * t + P], qk_rest[:, :, :], ACT.Copy).then_inc(cast2, 1)

            for t in range(NT):
                if t == 0:
                    act.wait_ge(normed, NT)
                copy_x(t)
                copy_xT(t)
                cast_first(t, t, 0, first=True)
                cast_second(t, t)
            act.wait_ge(normed, TILES)

            def exp(b, u):
                blk, j, q = unit(u)
                if u % 8 == 0:
                    act.wait_ge(pv_done, b * HALVES + blk - 2 + 1 + FREE_P)
                act.wait_ge(turned, b * UNITS + u + 1 + FREE_SC)
                act.activation(probs[:, blk % 2, j, :, P * (q % 2):P * (q % 2) + P],
                               bank_t[u % 2][:, :].rearrange("p (k q) -> p k q", k=NT), ACT.Exp).then_inc(exped, 1)

            def copy_ctx(b, blk):
                act.wait_ge(pv_done, b * HALVES + blk + 1 + FREE_P)
                act.wait_ge(ctx_turned, b * HALVES + blk - 2 + 1 + FREE_R)
                act.activation(ctx_raw[:, blk % 2, :], bank_c[blk % 2][:, 0:HALF], ACT.Copy).then_inc(ctx_out, 1)

            def copy_back(b, i):
                act.wait_ge(back_turned, b * 2 + i + 1 + FREE_1)
                act.wait_ge(wo_done, b * 2 + FREE_1)
                act.activation(ctxT[:, :, HALF * i:HALF * i + HALF],
                               bank_m[1 - i][:, :].rearrange("p (c n) -> p c n", c=NC), ACT.Copy).then_inc(back_out, 1)

            def batch(b, last):
                for u in range(UNITS):
                    exp(b, u)
                    if u % 8 == 6 and u >= 8:
                        copy_ctx(b, u // 8 - 1)
                    if not last:
                        for t, at in enumerate(SLICE_AT):
                            s = (b + 1) * NT + t
                            if u == at - 3:
                                copy_x(s)
                            if u == at:
                                copy_xT(s)
                            if u == at + 2:
                                cast_first(s, t, b + 1)
                            if u == at + 4:
                                cast_second(s, t)
                copy_ctx(b, HALVES - 1)
                copy_back(b, 0)
                copy_back(b, 1)

            with act.Fori(0, B - 1) as b:
                batch(b, False)
            batch(B - 1, True)

            act.wait_ge(aggr_done, 2 * TILES)
            act.activation(sd2[:, :], meanvar2[:, :, 1], ACT.Sqrt, bias=eps[:, 0:1]).then_inc(sd_done, 1)
            act.wait_ge(rows_in, 16 * 6)

            def copy_hT(b):
                for c in range(NC):
                    act.wait_ge(h_turned, b * NC + c + 1)
                    if c == 0:
                        act.wait_ge(ff1_done, b * NF)
                    act.activation(hT[:, c, :], bank_s[c][:, :], ACT.Identity, scale=g2_col[:, c:c + 1],
                                   bias=beta2_col[:, c:c + 1]).then_inc(hT_out, 1)

            def feed(b, last):
                for f in range(NF):
                    act.wait_ge(ff1_done, b * NF + f + 1)
                    if f == 0:
                        act.wait_ge(ff2_done, b * NT + FREE_1)
                    act.activation(gT[:, f, :], ff_bank(f)[:, :], ACT.Gelu_apprx_sigmoid, bias=b1_col[:, f:f + 1])\
                        .then_inc(gelu_done, 1)
                if not last:
                    copy_hT(b + 1)

            copy_hT(0)
            with act.Fori(0, B - 1) as b:
                feed(b, False)
            feed(B - 1, True)

        @block.tensor
        def _(pe):
            pe.wait_ge(wide_done, 1)
            pe.wait_ge(ada_in, 32)
            for b in range(B):
                for c in range(NC):
                    mm = pe.matmul((bank_s + bank_t)[b][:, :], emb_wide[:, c * B + b, :], w_ada_sb[:, c, :],
                                   start=(c == 0), stop=(c == NC - 1))
                mm.then_inc(emb_done, 1)

            def slice_turn(s, y_before):
                pe.wait_ge(x_copied, s + 1)
                pe.wait_ge(v_out, s)
                pe.wait_ge(y_done, y_before + FREE_1)
                for c in range(NC):
                    mm = pe.transpose(bank_m[1][:, P * c:P * c + P], x_now[:, P * c:P * c + P], ident)
                mm.then_inc(x_turned, 1)

            def slice_qk(s):
                pe.wait_ge(xT_out, s + 1)
                for m in range(4):
                    for c in range(NC):
                        mm = pe.matmul(bank_m[1][:, P * m:P * m + P], w_qk[:, c, P * m:P * m + P], xT[:, c, :],
                                       start=(c == 0), stop=(c == NC - 1))
                mm.then_inc(qk_proj, 1)

            def slice_v(s):
                pe.wait_ge(qk_out, s + 1)
                for c in range(NC):
                    mm = pe.matmul(bank_m[1][:, 0:D], xT[:, c, :], w_v[:, c, :], start=(c == 0), stop=(c == NC - 1))
                mm.then_inc(v_proj, 1)

            pe.wait_ge(proj_in, 16 * 6)
            pe.wait_ge(wscaled, 2)
            for t in range(NT):
                slice_turn(t, 0)
                slice_qk(t)
                slice_v(t)

            def qk(b, u):
                blk, j, q = unit(u)
                g = blk // 2
                pe.wait_ge(summed, b * UNITS + u - 2 + 1 + FREE_S)
                if u % 16 == 0:
                    pe.wait_ge(stacked[g % 2], (b * 2 + g // 2 + 1) * (MOVES * 16))
                pe.matmul(bank_s[u % 2][:, :], stack_q[:, g % 2, j, P * q:P * q + P], stack_k[:, g % 2, j, :],
                          start=True, stop=True).then_inc(qk_done, 1)

            def turn(b, u):
                pe.wait_ge(shifted, b * UNITS + u + 1)
                pe.wait_ge(exped, b * UNITS + u - 2 + 1 + FREE_T)
                for k in range(NT):
                    mm = pe.transpose(bank_t[u % 2][:, P * k:P * k + P], scores[:, u % NSC, P * k:P * k + P], ident)
                mm.then_inc(turned, 1)

            def pv(b, blk, k):
                if k == 0:
                    pe.wait_ge(exped, b * UNITS + 8 * blk + 8 + FREE_T)
                    pe.wait_ge(ctx_out, b * HALVES + blk - 2 + 1 + FREE_C)
                    pe.wait_ge(v_moved, b + 1)
                for j in range(4):
                    mm = pe.matmul(bank_c[blk % 2][VW * j:VW * j + VW, 0:HALF], V[:, k, 4 * (blk // 2) + j, :],
                                   probs[:, blk % 2, j, k, :], start=(k == 0), stop=(k == NT - 1))
                if k == NT - 1:
                    mm.then_inc(pv_done, 1)

            def ctx_turn(b, blk):
                pe.wait_ge(ctx_out, b * HALVES + blk + 1 + FREE_C)
                pe.wait_ge(ctx_norm, b * HALVES + blk + FREE_1)
                if blk == 0:
                    pe.wait_ge(y_done, b * 2 + FREE_1)
                for q in range(2):
                    mm = pe.transpose(bank_m[0][:, P * q:P * q + P], ctx_raw[:, blk % 2, P * q:P * q + P], ident)
                mm.then_inc(ctx_turned, 1)

            def back_turn(b, i):
                pe.wait_ge(ctx_norm, (b + 1) * HALVES - 1 + i + FREE_1)
                if i == 0:
                    pe.wait_ge(v_out, slice_back(b))
                for c in range(NC):
                    for q in range(2):
                        mm = pe.transpose(bank_m[1 - i][:, P * (2 * c + q):P * (2 * c + q) + P],
                                          ctx_tok[:, 2 * i + q, P * c:P * c + P], ident)
                mm.then_inc(back_turned, 1)

            def slice_back(b):
                return (b + 2) * NT if not isinstance(b, int) or b < B - 1 else B * NT

            def project_out(b, i):
                pe.wait_ge(back_out, b * 2 + i + 1)
                for q in range(2):
                    for c in range(NC):
                        at = P * (2 * i + q)
                        mm = pe.matmul(bank_m[1 - i][:, D * q:D * q + D], ctxT[:, c, at:at + P], w_o[:, c, :],
                                       start=(c == 0), stop=(c == NC - 1))
                mm.then_inc(wo_done, 1)

            def batch(b, last):
                for u in range(UNITS):
                    blk, p = u // 8, u % 8
                    if u + 2 < UNITS:
                        qk(b, u + 2)
                    elif not last:
                        qk(b + 1, u + 2 - UNITS)
                    if u > 0:
                        turn(b, u - 1)
                    if p == 1 and blk >= 2:
                        ctx_turn(b, blk - 2)
                    if 2 <= p < 6 and blk >= 1:
                        pv(b, blk - 1, p - 2)
                    if not last:
                        for t, at in enumerate(SLICE_AT):
                            s = (b + 1) * NT + t
                            if u == at:
                                slice_turn(s, b * 2)
                            if u == at + 1:
                                slice_qk(s)
                            if u == at + 3:
                                slice_v(s)
                turn(b, UNITS - 1)
                ctx_turn(b, HALVES - 2)
                for k in range(NT):
                    pv(b, HALVES - 1, k)
                back_turn(b, 0)
                ctx_turn(b, HALVES - 1)
                project_out(b, 0)
                back_turn(b, 1)
                project_out(b, 1)

            pe.wait_ge(row_done, 2 * B)
            qk(0, 0)
            qk(0, 1)
            with pe.Fori(0, B - 1) as b:
                batch(b, False)
            batch(B - 1, True)

            def turn_h(b):
                for c in range(NC):
                    for t in range(NT):
                        if c == 0:
                            pe.wait_ge(h_done, b * NT + t + 1)
                        if t == 0:
                            pe.wait_ge(hT_out, b * NC)
                        mm = pe.transpose(bank_s[c][:, P * t:P * t + P], h_now[:, t, P * c:P * c + P], ident)
                    mm.then_inc(h_turned, 1)

            def feed(b, last):
                pe.wait_ge(hT_out, (b + 1) * NC)
                for f in range(NF):
                    pe.wait_ge(gelu_done, b * NF + f - 4 + 1 + FREE_G)
                    for c in range(NC):
                        mm = pe.matmul(ff_bank(f)[:, :], w1_sb[:, c, P * f:P * f + P], hT[:, c, :],
                                       start=(c == 0), stop=(c == NC - 1))
                    mm.then_inc(ff1_done, 1)
                if not last:
                    turn_h(b + 1)
                for t in range(NT):
                    if t >= 2:
                        pe.wait_ge(o_done, b * NT + t - 1 + FREE_1)
                    else:
                        pe.wait_ge(o_done, b * NT + FREE_1)
                    for f in range(NF):
                        if t == 0:
                            pe.wait_ge(gelu_done, b * NF + f + 1 + FREE_G)
                        mm = pe.matmul(bank_m[t % 2][:, 0:D], gT[:, f, P * t:P * t + P], w2_sb[:, f, :],
                                       start=(f == 0), stop=(f == NF - 1))
                    mm.then_inc(ff2_done, 1)

            turn_h(0)
            pe.wait_ge(ffn_in, 32)
            with pe.Fori(0, B - 1) as b:
                feed(b, False)
            feed(B - 1, True)

        @block.vector
        def _(dve):
            for s, n in ((summed, FREE_S), (turned, FREE_SC), (exped, FREE_T), (pv_done, FREE_P), (ctx_out, FREE_C),
                         (ctx_turned, FREE_R), (gelu_done, FREE_G), (ctx_norm, FREE_1), (y_done, FREE_1), (wo_done, FREE_1),
                         (back_turned, FREE_1), (ff2_done, FREE_1), (o_done, FREE_1)):
                dve.sem_inc(s, n)
            steps = [0]

            def step(ins):
                steps[0] += 1
                ins.then_inc(angle_step, 1)
                dve.wait_ge(angle_step, steps[0])

            dve.wait_ge(angles_in, 16 * 6)
            step(dve.tensor_scalar(angle[:, SIN_E:SIN_E + B], t_int[:, :], 0.01, 4000.0, ALU.mult, ALU.mult))
            step(dve.tensor_scalar(angle[:, COS_E:COS_E + B], angle[:, SIN_E:SIN_E + B], cst[:, C_FREQ:C_FREQ + 1], None, ALU.mult))
            step(dve.tensor_copy(angle[:, SIN_E:SIN_E + B], angle[:, COS_E:COS_E + B]))
            step(dve.scalar_tensor_tensor(out=turns[:, :], in0=angle[:, :], scalar=INV_2PI,
                                          in1=cst[:, C_TURN:C_TURN + ANGLES], op0=ALU.mult, op1=ALU.add))
            step(dve.tensor_scalar(turns[:, :], turns[:, :], ROUND, None, ALU.add))
            step(dve.tensor_scalar(turns[:, :], turns[:, :], -ROUND, None, ALU.add))
            for part in (TWO_PI_A, TWO_PI_B, TWO_PI_C):
                in1 = angle[:, :]
                ins = dve.scalar_tensor_tensor(out=angle[:, :], in0=turns[:, :], scalar=-part, in1=in1,
                                               op0=ALU.mult, op1=ALU.add)
                if part != TWO_PI_C:
                    step(ins)
                else:
                    ins.then_inc(minus_done, 1)
                    dve.wait_ge(minus_done, 1)
            dve.tensor_tensor(angle[:, :], angle[:, :], cst[:, C_PHASE:C_PHASE + ANGLES], ALU.add).then_inc(minus_done, 1)
            dve.wait_ge(minus_done, 2)
            step(dve.tensor_scalar(angle[:, :], angle[:, :], -PI_IN, None, ALU.max))
            step(dve.tensor_scalar(angle[:, :], angle[:, :], PI_IN, None, ALU.min))
            dve.wait_ge(sin_done, 1)
            dve.tensor_scalar(minus[:, :], sincos[:, :], -1.0, None, ALU.mult).then_inc(minus_done, 1)
            dve.wait_ge(silu_done, 1)
            dve.tensor_copy(emb_wide, emb[:, :].rearrange("p (c o) -> p c o", o=1).broadcast_to([P, 8, P])).then_inc(wide_done, 1)
            dve.wait_ge(minus_done, 3)
            for b in range(B):
                for i, (to, fro, s) in enumerate(((0, 1, sincos[:, SIN_T + b:SIN_T + b + 1]), (1, 0, minus[:, SIN_T + b:SIN_T + b + 1]),
                                                  (2, 3, sincos[:, SIN_P + b:SIN_P + b + 1]), (3, 2, minus[:, SIN_P + b:SIN_P + b + 1]))):
                    if i % 2 == 0:
                        dve.wait_ge(cos_part, 2 * b + i // 2 + 1)
                    src, dst = (v[:, NT * b:NT * b + NT, :].rearrange("p t (n e) -> p (t n) e", e=4) for v in (x_raw, X))
                    dve.scalar_tensor_tensor(out=dst[:, :, to], in0=src[:, :, fro], scalar=s, in1=dst[:, :, to],
                                             op0=ALU.mult, op1=ALU.add).then_inc(rotated, 1)
            for i in range(TILES):
                if i % NT == 0:
                    dve.wait_ge(rotated, 4 * (i // NT) + 4)
                dve.bn_stats(stats[:, i, :], X[:, i, :]).then_inc(stat_done, 1)
            for i in range(TILES):
                dve.wait_ge(stat_done, i + 1)
                dve.bn_aggr(meanvar[:, i, :], stats[:, i, :]).then_inc(aggr_done, 1)
            for b in range(B):
                src = (bank_s + bank_t)[b]
                dve.wait_ge(emb_done, b + 1)
                if b == 0:
                    dve.wait_ge(ada_in, 32)
                dve.scalar_tensor_tensor(out=row_scale[:, b, 0:D], in0=src[:, 0:D], scalar=1.0, in1=b_ada_row[:, 0:D],
                                         op0=ALU.add, op1=ALU.add).then_inc(row_done, 1)
                dve.tensor_tensor(row_scale[:, b, D:2 * D], src[:, D:2 * D], b_ada_row[:, D:2 * D], ALU.add).then_inc(row_done, 1)
            dve.wait_ge(sd_done, 1)
            dve.reciprocal(rstd[:, :], sd[:, :]).then_inc(rstd_done, 1)
            dve.wait_ge(rstd_done, 1)
            dve.wait_ge(row_done, 2 * B)

            def norm_batch(b):
                for t in range(NT):
                    i = NT * b + t
                    dve.scalar_tensor_tensor(out=X[:, i, :], in0=X[:, i, :], scalar=meanvar[:, i, 0:1],
                                             in1=row_scale[:, b, 0:D], op0=ALU.subtract, op1=ALU.mult).then_inc(centred, 1)
                for t in range(NT):
                    i = NT * b + t
                    dve.wait_ge(centred, i + 1)
                    dve.scalar_tensor_tensor(out=X[:, i, :], in0=X[:, i, :], scalar=rstd[:, i:i + 1],
                                             in1=row_scale[:, b, D:2 * D], op0=ALU.mult, op1=ALU.add).then_inc(normed, 1)

            def qk_bias(s):
                dve.wait_ge(qk_proj, s + 1)
                dve.wait_ge(rest1, s)
                dve.wait_ge(cast1, s)
                dve.tensor_tensor(qk_full[:, :, :], bank_m[1][:, :].rearrange("p (m n) -> p m n", m=4),
                                  b_qk[:, :].rearrange("p (m o) -> p m o", o=1).broadcast_to([P, 4, P]), ALU.add)\
                    .then_inc(qk_out, 1)

            def v_bias(s, t, b):
                dve.wait_ge(v_proj, s + 1)
                if t == 0:
                    dve.wait_ge(v_moved, b)
                dve.tensor_tensor(V_next[:, t, :, 0:DH], bank_m[1][:, 0:D].rearrange("p (h w) -> p h w", h=H),
                                  bv_row[:, :].rearrange("p (h w) -> p h w", h=H), ALU.add).then_inc(v_out, 1)

            norm_batch(0)
            dve.wait_ge(wscaled, 2)
            dve.wait_ge(rows_in, 16 * 6)
            dve.wait_ge(ready, 3)
            for t in range(NT):
                qk_bias(t)
                v_bias(t, t, 0)
            for b in range(1, B):
                norm_batch(b)
            dve.wait_ge(normed, TILES)

            def await_sum(b, u):
                dve.wait_ge(qk_done, b * UNITS + u + 1)
                dve.wait_ge(masked, b * (UNITS // 2) + u // 2 + 1)
                dve.wait_ge(turned, b * UNITS + u - NSC + 1 + FREE_SC)

            def sum_max(b, u):
                c = u // 4
                dve.tensor_tensor_reduce(out=scores[:, u % NSC, :], in0=bank_s[u % 2][:, :],
                                         in1=ring[:, c % RING, u % 4 // 2, u % 2, :], scale=1.0, scalar=LOWEST,
                                         op0=ALU.add, op1=ALU.max, accum_out=row_max[:, u % NSC:u % NSC + 1]).then_inc(summed, 1)

            def shift(b, u):
                dve.wait_ge(summed, b * UNITS + u + 1 + FREE_S)
                if u + 2 < UNITS:
                    await_sum(b, u + 2)
                dve.tensor_scalar(scores[:, u % NSC, :], scores[:, u % NSC, :], row_max[:, u % NSC:u % NSC + 1], None,
                                  ALU.subtract).then_inc(shifted, 1)

            def denominator(b, blk):
                dve.wait_ge(ctx_turned, b * HALVES + blk + 1 + FREE_R)
                dve.reciprocal(ctx_sum[:, :, :], bank_m[0][:, 0:HALF].rearrange("p (q h w) -> p q h w", q=2, h=4)[:, :, :, ONE])\
                    .then_inc(ctx_recip, 1)

            def divide(b, blk):
                dve.wait_ge(ctx_recip, b * HALVES + blk + 1)
                if blk == 0:
                    dve.wait_ge(back_turned, b * 2 + FREE_1)
                q0, g = 2 * (blk % 2), blk // 2
                for q in range(2):
                    src = bank_m[0][:, P * q:P * q + P].rearrange("p (h w) -> p h w", h=4)[:, :, 0:DH]
                    ins = dve.tensor_tensor(ctx_tok[:, q0 + q, 4 * DH * g:4 * DH * (g + 1)].rearrange("p (h w) -> p h w", h=4),
                                            src, ctx_sum[:, q, :].rearrange("p (h o) -> p h o", o=1).broadcast_to([P, 4, DH]),
                                            ALU.mult)
                ins.then_inc(ctx_norm, 1)

            def residual(b, i):
                src = bank_m[1 - i][:, :].rearrange("p (q d) -> p q d", q=2)
                dst = X[:, bass.ds(b * NT + 2 * i, 2), :]
                dve.wait_ge(wo_done, b * 2 + i + 1 + FREE_1)
                dve.tensor_tensor(dst, src, dst, ALU.add).then_inc(wo_bias, 1)
                dve.wait_ge(wo_bias, b * 2 + i + 1)
                dve.tensor_tensor(dst, dst, bo_row[:, :].rearrange("p (o d) -> p o d", o=1).broadcast_to([P, 2, D]), ALU.add)\
                    .then_inc(y_done, 1)

            def residual_stats(b, i):
                dve.wait_ge(y_done, b * 2 + i + 1 + FREE_1)
                for q in range(2):
                    at = b * NT + 2 * i + q
                    dve.bn_stats(stats2[:, bass.ds(at, 1), :].rearrange("p o s -> p (o s)"),
                                 X[:, bass.ds(at, 1), :].rearrange("p o s -> p (o s)")).then_inc(stat_done, 1)

            def batch(b, last):
                for u in range(UNITS):
                    blk, p = u // 8, u % 8
                    if u < 2:
                        await_sum(b, u)
                        dve.memset(dve_spare[:, u:u + 1], 0.0)
                    sum_max(b, u)
                    if u > 0:
                        shift(b, u - 1)
                    if u == 2:
                        dve.wait_ge(v_out, (b + 1) * NT)
                        dve.wait_ge(pv_done, b * HALVES + FREE_P)
                        dve.tensor_copy(V[:, :, :, :], V_next[:, :, :, :]).then_inc(v_moved, 1)
                    if p == 3 and blk >= 2:
                        denominator(b, blk - 2)
                    if p == 4 and blk >= 2:
                        divide(b, blk - 2)
                    if not last:
                        for t, at in enumerate(SLICE_AT):
                            s = (b + 1) * NT + t
                            if u == at + 2:
                                qk_bias(s)
                            if u == at + 4:
                                v_bias(s, t, b + 1)
                shift(b, UNITS - 1)
                denominator(b, HALVES - 2)
                divide(b, HALVES - 2)
                denominator(b, HALVES - 1)
                divide(b, HALVES - 1)
                residual(b, 0)
                residual(b, 1)
                residual_stats(b, 0)
                residual_stats(b, 1)

            with dve.Fori(0, B - 1) as b:
                batch(b, False)
            batch(B - 1, True)

            for i in range(TILES):
                dve.wait_ge(stat_done, TILES + i + 1)
                dve.bn_aggr(meanvar2[:, i, :], stats2[:, i, :]).then_inc(aggr_done, 1)
            dve.wait_ge(sd_done, 2)
            dve.reciprocal(rstd2[:, :], sd2[:, :]).then_inc(rstd_done, 1)
            dve.wait_ge(rstd_done, 2)

            def normalise(b):
                dve.wait_ge(h_turned, b * NC)
                for t in range(NT):
                    at = b * NT + t
                    dve.tensor_scalar(h_now[:, t, :], X[:, bass.ds(at, 1), :].rearrange("p o d -> p (o d)"),
                                      meanvar2[:, bass.ds(at, 1), 0], rstd2[:, bass.ds(at, 1)],
                                      ALU.subtract, ALU.mult).then_inc(h_done, 1)

            def finish(b):
                dve.wait_ge(yb_done, b + 1)
                for t in range(NT):
                    dve.wait_ge(ff2_done, b * NT + t + 1 + FREE_1)
                    dve.tensor_tensor(o_sb[:, b % 2, t, :], bank_m[t % 2][:, 0:D], yb[:, t, :], ALU.add).then_inc(o_done, 1)

            normalise(0)
            for b in range(B):
                if b + 1 < B:
                    normalise(b + 1)
                if b >= 2:
                    dve.wait_ge(out_in[b % 2], 16 * NT * (b // 2))
                finish(b)



_INS = ["x", "condB_theta", "condB_phi", "itok_B_34_63", "fside_Bx16xSxS_0", "mask_Bx1xSxS_bk0",
        "L1_cond_W_ada", "L1_cond_b_ada", "L1_cond_Wq", "L1_cond_bq", "L1_cond_Wk", "L1_cond_bk",
        "L1_cond_Wv", "L1_cond_bv", "L1_cond_Wo", "L1_cond_bo", "L1_cond_W1", "L1_cond_b1",
        "L1_cond_W2", "L1_cond_b2", "L1_cond_g2", "L1_cond_beta2"]

_COLUMNS = ["bq", "bk", "b1", "g2", "beta2"]


def kernel(**inputs):
    import concourse.bacc as bacc
    from concourse.bass_utils import run_bass_kernel_spmd as run

    nc = bacc.Bacc("TRN2", target_bir_lowering=False, num_devices=1)
    arrays, args = {}, []
    for name in _INS + ["constants"]:
        a = np.ascontiguousarray(constants() if name == "constants" else inputs[name])
        if a.dtype == np.bool_:
            a = a.view(np.uint32)
        if name.removeprefix("L1_cond_") in _COLUMNS:
            a = np.ascontiguousarray(a.reshape(-1, P).T)
        arrays[f"in_{name}"] = a
        args.append(nc.dram_tensor(f"in_{name}", a.shape, mybir.dt.from_np(a.dtype), kind="ExternalInput").ap())
    out = nc.dram_tensor("out", (B, S, D), F32, kind="ExternalOutput").ap()
    rotate_then_attend_then_feed_forward(nc, *args, out)
    r = run(nc, [arrays], core_ids=[0])
    return r.results[0]["out"]
```

```python
from contextlib import ExitStack
import math

import numpy as np

import concourse.bass as bass
from concourse import mybir

F32 = mybir.dt.float32
BF16 = mybir.dt.bfloat16
I32 = mybir.dt.int32
U8 = mybir.dt.uint8
U32 = mybir.dt.uint32
ALU = mybir.AluOpType
ACT = mybir.ActivationFunctionType

B, S, D, H, DH, F = 4, 512, 256, 16, 16, 1024
P = 128
NT = S // P
TILES = B * NT
NC = D // P
NF = F // P
QUADS = H // 4
HALF = 2 * P
HALVES = 2 * QUADS
UNITS = 8 * HALVES
LOADS = UNITS // 4
RING = 4
NSC = 4
VW = 32
ONE = DH

EPS = 1e-5
MASKED = -1e30
LOWEST = -3.0e38
INV_2PI = 1.0 / (2.0 * math.pi)
ROUND = 12582912.0
TWO_PI_A = 6.28125
TWO_PI_B = float(np.float32(np.round((2.0 * math.pi - TWO_PI_A) * 2**22) / 2**22))
TWO_PI_C = 2.0 * math.pi - TWO_PI_A - TWO_PI_B
PI_IN = 3.1415925

TERMS = [(0, 0), (0, 1), (1, 0), (1, 1), (0, 2), (2, 0)]
ROWS = len(TERMS) * DH
MOVES = 2 * len(TERMS)

SIN_E, COS_E, COS_T, SIN_T, COS_P, SIN_P, ANGLES = 0, 4, 8, 12, 16, 20, 24
C_ID, C_FREQ, C_TURN, C_PHASE, C_ALL = 0, P, P + 1, P + 1 + 24, P + 1 + 48

SLICE_AT = [19, 26, 33, 40]
OUT_AT = [6, 14]
ON_PE = 3
POOL_MASKS = 3 * HALVES


def constants():
    c = np.zeros((P, C_ALL), np.float32)
    c[:, C_ID:C_ID + P] = np.eye(P, dtype=np.float32)
    step = np.float32(-math.log(10000.0) / (P - 1))
    c[:, C_FREQ] = np.exp(np.arange(P, dtype=np.float32) * step)
    for at in (COS_E, COS_T, COS_P):
        c[:, C_TURN + at:C_TURN + at + 4] = 0.25
        c[:, C_PHASE + at:C_PHASE + at + 4] = math.pi / 2
    return c


def rotate_then_attend_then_feed_forward(nc, x, theta, phi, timestep, bias, mask, w_ada, b_ada, wq, bq, wk, bk,
                                         wv, bv, wo, bo, w1, b1, w2, b2, g2, beta2, const, out):
    ctx = ExitStack()
    with ctx:
        def sb(name, shape, dt=F32):
            return ctx.enter_context(nc.sbuf_tensor(name, shape, dt))

        def sem(name):
            return ctx.enter_context(nc.semaphore(name))

        part_rows = nc.dram_tensor("part_rows", (3, 4, P, S), BF16, kind="Internal").ap()

        bank_s = [ctx.enter_context(nc.psum_tensor(f"bank_s{i}", [P, S], F32)) for i in range(2)]
        bank_t = [ctx.enter_context(nc.psum_tensor(f"bank_t{i}", [P, S], F32)) for i in range(2)]
        bank_c = [ctx.enter_context(nc.psum_tensor(f"bank_c{i}", [P, S], F32)) for i in range(2)]
        bank_m = [ctx.enter_context(nc.psum_tensor(f"bank_m{i}", [P, S], F32)) for i in range(2)]

        ring = sb("ring", [P, RING, 2, 2, S])
        probs = sb("probs", [P, 2, 4, NT, HALF])
        scores = sb("scores", [P, NSC, S])
        stack_q = sb("stack_q", [ROWS, 2, 4, S], BF16)
        stack_k = sb("stack_k", [ROWS, 2, 4, S], BF16)
        parts = sb("parts", [P, 3, 4, S], BF16)
        qk_full = sb("qk_full", [P, 4, P])
        qk_rest = sb("qk_rest", [P, 4, P])
        x_now = sb("x_now", [P, 2, D])
        xT = sb("xT", [P, 2, NC, P])
        X = sb("X", [P, TILES, D])
        V = sb("V", [P, NT, H, VW])
        V_next = sb("V_next", [P, NT, H, VW])
        mask_add = sb("mask_add", [P, TILES, S], BF16)
        ctx_raw = sb("ctx_raw", [P, 2, HALF])
        ctx_sum = sb("ctx_sum", [P, 2, 4])
        ctx_tok = sb("ctx_tok", [P, NT, D])
        ctxT = sb("ctxT", [P, NC, S])
        cst = sb("cst", [P, C_ALL])
        w_qk = sb("w_qk", [P, NC, 2 * D])
        w_v = sb("w_v", [P, NC, D])
        w_o = sb("w_o", [P, NC, D])
        b_qk = sb("b_qk", [P, 4])
        bv_row = sb("bv_row", [P, D])
        bo_row = sb("bo_row", [P, D])
        b2_row = sb("b2_row", [P, D])
        b1_col = sb("b1_col", [P, NF])
        g2_col = sb("g2_col", [P, NC])
        beta2_col = sb("beta2_col", [P, NC])
        eps = sb("eps", [P, 1])
        pool_spare = sb("pool_spare", [P, RING])
        dve_spare = sb("dve_spare", [P, 2])
        t_int = sb("t_int", [P, B], I32)
        angle = sb("angle", [P, ANGLES])
        turns = sb("turns", [P, ANGLES])
        sincos = sb("sincos", [P, ANGLES])
        minus = sb("minus", [P, ANGLES])
        emb = sb("emb", [P, 8])
        stats = sb("stats", [P, TILES, 6])
        meanvar = sb("meanvar", [P, TILES, 2])
        stats2 = sb("stats2", [P, TILES, 6])
        meanvar2 = sb("meanvar2", [P, TILES, 2])
        sd = sb("sd", [P, TILES])
        rstd = sb("rstd", [P, TILES])
        sd2 = sb("sd2", [P, TILES])
        rstd2 = sb("rstd2", [P, TILES])
        ident_half = sb("ident_half", [P, P], BF16)
        row_scale = sb("row_scale", [P, B, 2 * D])
        row_max = sb("row_max", [P, NSC])
        ident = cst[:, C_ID:C_ID + P]

        flat = probs[:, :, :, :, :].rearrange("p a h k q -> p (a h k q)")
        x_raw = flat[:, 0:TILES * D].rearrange("p (t d) -> p t d", t=TILES)
        mask_words = flat[:, TILES * D:TILES * D + TILES * S // 4].bitcast(U32)
        mask_raw = mask_words.bitcast(U8).rearrange("p (t k) -> p t k", t=TILES)
        wide = V[:, :, :, :].rearrange("p a h w -> p (a h w)")
        emb_wide = wide[:, 0:8 * P].rearrange("p (c n) -> p c n", c=8)
        vn = V_next[:, :, :, :].rearrange("p a h w -> p (a h w)")
        w_ada_sb = ctxT[:, :, :]
        b_ada_row = ctx_raw[:, :, :].rearrange("p a n -> p (a n)")
        rflat = ring[:, :, :, :, :].rearrange("p r h t k -> p (r h t k)")
        w1_sb = rflat[:, 0:NC * F].rearrange("p (c f) -> p c f", c=NC)
        w2_sb = rflat[:, NC * F:NC * F + NF * D].rearrange("p (c d) -> p c d", c=NF)
        gT = rflat[:, 4096:8192].rearrange("p (c n) -> p c n", c=NF)
        h_now = flat[:, 0:1024].rearrange("p (t d) -> p t d", t=NT)
        hT = flat[:, 1024:2048].rearrange("p (c n) -> p c n", c=NC)
        yb = flat[:, 2048:3072].rearrange("p (t d) -> p t d", t=NT)
        o_sb = flat[:, 4096:6144].rearrange("p (a t d) -> p a t d", a=2, t=NT)

        angles_in = sem("angles_in")
        x_in = [sem(f"x_in{b}") for b in range(B)]
        mask_in = sem("mask_in")
        ada_in = sem("ada_in")
        proj_in = sem("proj_in")
        rows_in = sem("rows_in")
        ffn_in = sem("ffn_in")
        bias_in = [sem(f"bias_in{i}") for i in range(RING)]
        stored = sem("stored")
        stacked = [sem(f"stacked{i}") for i in range(2)]
        out_in = [sem(f"out_in{i}") for i in range(2)]
        ready = sem("ready")
        angle_step = sem("angle_step")
        sin_done = sem("sin_done")
        silu_done = sem("silu_done")
        wide_done = sem("wide_done")
        emb_done = sem("emb_done")
        row_done = sem("row_done")
        minus_done = sem("minus_done")
        cos_part = sem("cos_part")
        rotated = sem("rotated")
        stat_done = sem("stat_done")
        aggr_done = sem("aggr_done")
        sd_done = sem("sd_done")
        rstd_done = sem("rstd_done")
        centred = sem("centred")
        normed = sem("normed")
        mask_done = sem("mask_done")
        wscaled = sem("wscaled")
        x_copied = sem("x_copied")
        x_turned = sem("x_turned")
        xT_out = sem("xT_out")
        qk_proj = sem("qk_proj")
        qk_out = sem("qk_out")
        v_proj = sem("v_proj")
        v_out = sem("v_out")
        cast1 = sem("cast1")
        rest1 = sem("rest1")
        cast2 = sem("cast2")
        rest2 = sem("rest2")
        v_moved = sem("v_moved")
        masked = sem("masked")
        qk_done = sem("qk_done")
        summed = sem("summed")
        shifted = sem("shifted")
        turned = sem("turned")
        exped = sem("exped")
        pv_done = sem("pv_done")
        ctx_out = sem("ctx_out")
        ctx_turned = sem("ctx_turned")
        ctx_recip = sem("ctx_recip")
        ctx_norm = sem("ctx_norm")
        back_turned = sem("back_turned")
        back_out = sem("back_out")
        wo_done = sem("wo_done")
        wo_bias = sem("wo_bias")
        y_done = sem("y_done")
        h_done = sem("h_done")
        h_turned = sem("h_turned")
        hT_out = sem("hT_out")
        ff1_done = sem("ff1_done")
        gelu_done = sem("gelu_done")
        ff2_done = sem("ff2_done")
        yb_done = sem("yb_done")
        o_done = sem("o_done")

        FREE_S, FREE_SC, FREE_T, FREE_P, FREE_C, FREE_R, FREE_G, FREE_1 = 2, NSC, 2, 2, 2, 2, 4, 1

        def unit(u):
            blk, j, q = u // 8, u % 8 // 2, u % 2
            return blk, j, 2 * (blk % 2) + q

        def ff_bank(f):
            return (bank_t + bank_c)[f % 4]

        block = ctx.enter_context(nc.Block())

        @block.sync
        def _(sp):
            sp.dma_start(cst[:, :], const).then_inc(angles_in, 16)
            for src, at in ((timestep, None), (theta, COS_T), (theta, SIN_T), (phi, COS_P), (phi, SIN_P)):
                dst = t_int[:, :] if at is None else angle[:, at:at + B]
                sp.dma_start(dst, src.rearrange("(o b) -> o b", o=1).broadcast_to([P, B])).then_inc(angles_in, 16)
            sp.dma_start(x_raw[:, 0:NT, :], x[0].rearrange("(t p) d -> p t d", p=P)).then_inc(x_in[0], 16)
            sp.dma_start(w_ada_sb, w_ada.rearrange("(c p) n -> p c n", p=P)).then_inc(ada_in, 16)
            sp.dma_start(b_ada_row, b_ada.rearrange("(o n) -> o n", o=1).broadcast_to([P, 2 * D])).then_inc(ada_in, 16)
            for w, at in ((wq, 0), (wk, D)):
                sp.dma_start(w_qk[:, :, at:at + D], w.rearrange("(c p) n -> p c n", p=P)).then_inc(proj_in, 16)
            sp.dma_start(w_v[:, :, :], wv.rearrange("(c p) n -> p c n", p=P)).then_inc(proj_in, 16)
            sp.dma_start(w_o[:, :, :], wo.rearrange("(c p) n -> p c n", p=P)).then_inc(proj_in, 16)
            for v, at in ((bq, 0), (bk, 2)):
                sp.dma_start(b_qk[:, at:at + 2], v).then_inc(proj_in, 16)
            sp.dma_start(mask_words.rearrange("p (t k) -> p t k", t=TILES), mask.rearrange("b o (t p) k -> p (b o t) k", p=P)).then_inc(mask_in, 16)
            for b in range(1, B):
                sp.dma_start(x_raw[:, NT * b:NT * b + NT, :], x[b].rearrange("(t p) d -> p t d", p=P)).then_inc(x_in[b], 16)
            for v, row in ((bv, bv_row), (bo, bo_row), (b2, b2_row)):
                sp.dma_start(row[:, :], v.rearrange("(o n) -> o n", o=1).broadcast_to([P, D])).then_inc(rows_in, 16)
            sp.dma_start(b1_col[:, :], b1).then_inc(rows_in, 16)
            sp.dma_start(g2_col[:, :], g2).then_inc(rows_in, 16)
            sp.dma_start(beta2_col[:, :], beta2).then_inc(rows_in, 16)

            def load_bias(b, c, first=False):
                if not first:
                    sp.wait_ge(summed, b * UNITS + 4 * (c - RING) + 4 + FREE_S)
                blk, h = c // 2, 4 * (c // 4) + 2 * (c % 2)
                q0 = HALF * (blk % 2)
                src = bias[b] if first else bias[bass.ds(b, 1)].rearrange("o h q k -> (o h) q k")
                for i in range(2):
                    sp.dma_start(ring[:, c % RING, i, :, :], src[h + i, q0:q0 + HALF, :].rearrange("(t p) k -> p t k", p=P))\
                        .then_inc(bias_in[c % RING], 16)

            def await_all(*pairs):
                pairs = [(s, n if isinstance(n, int) else sp.snap(n)) for s, n in pairs]
                for s, n in pairs:
                    sp.wait_ge(s, n)

            def store_parts(b):
                split = NT * (b + 1)
                before = [] if isinstance(b, int) and b == 0 else [(stacked[i], b * (2 * MOVES * 16)) for i in range(2)]
                await_all((rest2, split), (cast2, split), *before)
                for i in range(3):
                    sp.dma_start(part_rows[i].rearrange("m p n -> p m n"), parts[:, i, :, :]).then_inc(stored, 16)

            def stack(b, g, first=False):
                if not first:
                    sp.wait_ge(qk_done, b * UNITS + 16 * (g - 1))
                if g == 0:
                    sp.wait_ge(stored, b * 48 + 48)
                r = 64 * (g % 2)
                for t, pair in enumerate(TERMS):
                    for dst, part, m in ((stack_q, pair[0], g // 2), (stack_k, pair[1], 2 + g // 2)):
                        sp.dma_start(dst[DH * t:DH * t + DH, g % 2, :, :],
                                     part_rows[part, m, r:r + 64, :].rearrange("(h d) n -> d h n", h=4))\
                            .then_inc(stacked[g % 2], 16)

            for c in range(RING):
                load_bias(0, c, first=True)
            store_parts(0)
            stack(0, 0, first=True)
            stack(0, 1, first=True)

            def batch(b, last):
                for c in range(RING, LOADS + RING):
                    if c < LOADS:
                        load_bias(b, c)
                    elif not last:
                        load_bias(b + 1, c - LOADS)
                    if c == 6:
                        stack(b, 2)
                    if c == 10:
                        stack(b, 3)
                    if c == 15 and not last:
                        store_parts(b + 1)
                        stack(b + 1, 0)
                if not last:
                    stack(b + 1, 1)

            with sp.Fori(0, B - 1) as b:
                batch(b, False)
            batch(B - 1, True)

            sp.wait_ge(summed, B * UNITS + FREE_S)
            sp.dma_start(w1_sb, w1.rearrange("(c p) f -> p c f", p=P)).then_inc(ffn_in, 16)
            sp.dma_start(w2_sb, w2.rearrange("(c p) d -> p c d", p=P)).then_inc(ffn_in, 16)
            for b in range(B):
                for t in range(NT):
                    sp.wait_ge(o_done, NT * b + t + 1 + FREE_1)
                    sp.dma_start(out[b, P * t:P * t + P, :], o_sb[:, b % 2, t, :]).then_inc(out_in[b % 2], 16)
            for i in range(2):
                sp.wait_ge(out_in[i], 16 * TILES // 2)

        @block.gpsimd
        def _(pool):
            pool.memset(eps[:, :], EPS).then_inc(ready, 1)
            pool.memset(V_next[:, :, :, :], 0.0).then_inc(ready, 1)
            pool.wait_ge(ready, 2)
            pool.memset(V_next[:, :, :, ONE:ONE + 1], 1.0).then_inc(ready, 1)
            pool.wait_ge(angles_in, 16 * 6)
            pool.tensor_copy(ident_half[:, :], ident).then_inc(ready, 1)

            def mask_bias(b, c, h):
                if h == 0:
                    pool.wait_ge(bias_in[c % RING], (b * (LOADS // RING) + c // RING + 1) * 32)
                    pool.tensor_tensor(pool_spare[:, c % RING:c % RING + 1], eps[:, :], eps[:, :], ALU.add)
                q = 2 * (c // 2 % 2)
                src = ring[:, c % RING, h, :, :]
                pool.tensor_tensor(src, src, mask_add[:, bass.ds(b * NT + q, 2), :], ALU.add).then_inc(masked, 1)

            def first_rest(s, t):
                pool.wait_ge(qk_out, s + 1)
                pool.wait_ge(cast1, s + 1)
                pool.wait_ge(cast2, s)
                pool.wait_ge(rest2, s)
                pool.tensor_tensor(qk_rest[:, :, :], qk_full[:, :, :], parts[:, 0, :, P * t:P * t + P], ALU.subtract)\
                    .then_inc(rest1, 1)

            def second_rest(s, t):
                pool.wait_ge(rest1, s + 1)
                pool.wait_ge(cast2, s + 1)
                pool.tensor_tensor(parts[:, 2, :, P * t:P * t + P], qk_rest[:, :, :], parts[:, 1, :, P * t:P * t + P],
                                   ALU.subtract).then_inc(rest2, 1)

            def mask_load(b, c):
                for h in range(2):
                    if 2 * (c % 2) + h != ON_PE:
                        mask_bias(b, c, h)

            pool.wait_ge(mask_done, 1)
            for c in range(2):
                mask_load(0, c)
            for t in range(NT):
                first_rest(t, t)
                second_rest(t, t)
            pool.wait_ge(mask_done, 2)

            def batch(b, last):
                for c in range(2, LOADS + 2):
                    if c < LOADS:
                        mask_load(b, c)
                    elif not last:
                        mask_load(b + 1, c - LOADS)
                    for t, at in enumerate(SLICE_AT):
                        if not last:
                            if c == at // 4 + 2:
                                first_rest((b + 1) * NT + t, t)
                            if c == at // 4 + 3:
                                second_rest((b + 1) * NT + t, t)

            with pool.Fori(0, B - 1) as b:
                batch(b, False)
            batch(B - 1, True)

            pool.wait_ge(rows_in, 16 * 6)
            with pool.Fori(0, B) as b:
                pool.wait_ge(y_done, B * 2 + FREE_1)
                pool.wait_ge(o_done, b * NT + FREE_1)
                pool.tensor_tensor(yb, X[:, bass.ds(b * NT, NT), :],
                                   b2_row[:, :].rearrange("p (o d) -> p o d", o=1).broadcast_to([P, NT, D]),
                                   ALU.add).then_inc(yb_done, 1)

        @block.scalar
        def _(act):
            act.wait_ge(angle_step, 10)
            act.activation(sincos[:, :], angle[:, :], ACT.Sin).then_inc(sin_done, 1)
            act.wait_ge(sin_done, 1)
            act.activation(emb[:, :], sincos[:, SIN_E:COS_E + B], ACT.Silu).then_inc(silu_done, 1)
            def cosines(b):
                act.wait_ge(x_in[b], 16)
                for pair, at in ((0, COS_T), (2, COS_P)):
                    src, dst = (v[:, NT * b:NT * b + NT, :].rearrange("p t (n e) -> p (t n) e", e=4)[:, :, pair:pair + 2]
                                for v in (x_raw, X))
                    act.activation(dst, src, ACT.Copy, scale=sincos[:, at + b:at + b + 1]).then_inc(cos_part, 1)
            def deviations(lo, hi):
                act.wait_ge(aggr_done, hi)
                act.activation(sd[:, lo:hi], meanvar[:, lo:hi, 1], ACT.Sqrt, bias=eps[:, 0:1]).then_inc(sd_done, 1)

            def masks(lo, hi):
                act.activation(mask_add[:, lo:hi, :], mask_raw[:, lo:hi, :], ACT.Copy, scale=MASKED).then_inc(mask_done, 1)

            cosines(0)
            act.wait_ge(ready, 1)
            deviations(0, NT)
            act.wait_ge(proj_in, 16 * 6)
            act.activation(w_qk[:, :, 0:D], w_qk[:, :, 0:D], ACT.Copy, scale=DH ** -0.5).then_inc(wscaled, 1)
            act.activation(b_qk[:, 0:2], b_qk[:, 0:2], ACT.Copy, scale=DH ** -0.5).then_inc(wscaled, 1)

            def copy_x(s, t):
                if not isinstance(s, int) or s > 1:
                    act.wait_ge(x_turned, s - 1)
                src = X[:, bass.ds(s, 1), :].rearrange("p o d -> p (o d)")
                act.activation(x_now[:, t % 2, :], src, ACT.Copy).then_inc(x_copied, 1)

            def copy_xT(s, t, bank):
                act.wait_ge(x_turned, s + 1)
                if not isinstance(s, int) or s > 1:
                    act.wait_ge(v_proj, s - 1)
                act.activation(xT[:, t % 2, :, :], bank[:, 0:NC * P].rearrange("p (c n) -> p c n", c=NC), ACT.Copy)\
                    .then_inc(xT_out, 1)

            def cast_first(s, t, b, first=False):
                act.wait_ge(qk_out, s + 1)
                if t == 0 and not first:
                    act.wait_ge(stored, b * 48)
                act.activation(parts[:, 0, :, P * t:P * t + P], qk_full[:, :, :], ACT.Copy).then_inc(cast1, 1)

            def cast_second(s, t):
                act.wait_ge(rest1, s + 1)
                act.activation(parts[:, 1, :, P * t:P * t + P], qk_rest[:, :, :], ACT.Copy).then_inc(cast2, 1)

            act.wait_ge(normed, NT)
            for t in range(2):
                copy_x(t, t)
            for t in range(2):
                copy_xT(t, t, bank_m[t % 2])
            act.wait_ge(mask_in, 16)
            masks(0, NT)
            for t in range(NT):
                cast_first(t, t, 0, first=True)
                if t + 2 < NT:
                    copy_x(t + 2, t + 2)
                cast_second(t, t)
                if t + 2 < NT:
                    copy_xT(t + 2, t + 2, bank_m[t % 2])
            for b in range(1, B):
                cosines(b)
            deviations(NT, TILES)
            masks(NT, TILES)

            def exp(b, u):
                blk, j, q = unit(u)
                if u % 8 == 0:
                    act.wait_ge(pv_done, b * HALVES + blk - 2 + 1 + FREE_P)
                act.wait_ge(turned, b * UNITS + u + 1 + FREE_SC)
                act.activation(probs[:, blk % 2, j, :, P * (q % 2):P * (q % 2) + P],
                               bank_t[u % 2][:, :].rearrange("p (k q) -> p k q", k=NT), ACT.Exp).then_inc(exped, 1)

            def copy_ctx(b, blk):
                act.wait_ge(pv_done, b * HALVES + blk + 1 + FREE_P)
                act.wait_ge(ctx_turned, b * HALVES + blk - 2 + 1 + FREE_R)
                act.activation(ctx_raw[:, blk % 2, :], bank_c[blk % 2][:, 0:HALF], ACT.Copy).then_inc(ctx_out, 1)

            def copy_back(b, i):
                act.wait_ge(back_turned, b * 2 + i + 1 + FREE_1)
                act.wait_ge(wo_done, b * 2 + FREE_1)
                act.activation(ctxT[:, :, HALF * i:HALF * i + HALF],
                               bank_m[1][:, :].rearrange("p (c n) -> p c n", c=NC), ACT.Copy).then_inc(back_out, 1)

            def batch(b, first, last):
                for u in range(UNITS):
                    exp(b, u)
                    if u % 8 == 6:
                        if u >= 8:
                            copy_ctx(b, u // 8 - 1)
                        elif not first:
                            copy_ctx(b - 1, HALVES - 1)
                    if not first and u in (OUT_AT[0], OUT_AT[1]):
                        copy_back(b - 1, OUT_AT.index(u))
                    if not last:
                        for t, at in enumerate(SLICE_AT):
                            s = (b + 1) * NT + t
                            if u == at - 4:
                                if t == 0 and first:
                                    act.wait_ge(normed, TILES)
                                copy_x(s, t)
                            if u == at - 1:
                                copy_xT(s, t, bank_m[1])
                            if u == at + 1:
                                cast_first(s, t, b + 1)
                            if u == at + 3:
                                cast_second(s, t)

            batch(0, True, False)
            with act.Fori(1, B - 1) as b:
                batch(b, False, False)
            batch(B - 1, False, True)
            copy_ctx(B - 1, HALVES - 1)
            copy_back(B - 1, 0)
            copy_back(B - 1, 1)

            act.wait_ge(aggr_done, 2 * TILES)
            act.activation(sd2[:, :], meanvar2[:, :, 1], ACT.Sqrt, bias=eps[:, 0:1]).then_inc(sd_done, 1)
            act.wait_ge(rows_in, 16 * 6)

            def copy_hT(b):
                for c in range(NC):
                    act.wait_ge(h_turned, b * NC + c + 1)
                    if c == 0:
                        act.wait_ge(ff1_done, b * NF)
                    act.activation(hT[:, c, :], bank_s[c][:, :], ACT.Identity, scale=g2_col[:, c:c + 1],
                                   bias=beta2_col[:, c:c + 1]).then_inc(hT_out, 1)

            def feed(b, last):
                for f in range(NF):
                    act.wait_ge(ff1_done, b * NF + f + 1)
                    if f == 0:
                        act.wait_ge(ff2_done, b * NT + FREE_1)
                    act.activation(gT[:, f, :], ff_bank(f)[:, :], ACT.Gelu_apprx_sigmoid, bias=b1_col[:, f:f + 1])\
                        .then_inc(gelu_done, 1)
                if not last:
                    copy_hT(b + 1)

            copy_hT(0)
            with act.Fori(0, B - 1) as b:
                feed(b, False)
            feed(B - 1, True)

        @block.tensor
        def _(pe):
            pe.wait_ge(wide_done, 1)
            pe.wait_ge(ada_in, 32)
            for b in range(B):
                for c in range(NC):
                    mm = pe.matmul((bank_s + bank_t)[b][:, :], emb_wide[:, c * B + b, :], w_ada_sb[:, c, :],
                                   start=(c == 0), stop=(c == NC - 1))
                mm.then_inc(emb_done, 1)

            def slice_turn(s, t, bank, y_before):
                pe.wait_ge(x_copied, s + 1)
                if y_before is None:
                    if s > 1:
                        pe.wait_ge(v_out, s - 1)
                else:
                    pe.wait_ge(v_out, s)
                    pe.wait_ge(y_done, y_before + FREE_1)
                for c in range(NC):
                    mm = pe.transpose(bank[:, P * c:P * c + P], x_now[:, t % 2, P * c:P * c + P], ident)
                mm.then_inc(x_turned, 1)

            def slice_qk(s, t, bank):
                pe.wait_ge(xT_out, s + 1)
                for m in range(4):
                    for c in range(NC):
                        mm = pe.matmul(bank[:, P * m:P * m + P], w_qk[:, c, P * m:P * m + P], xT[:, t % 2, c, :],
                                       start=(c == 0), stop=(c == NC - 1))
                mm.then_inc(qk_proj, 1)

            def slice_v(s, t, bank):
                pe.wait_ge(qk_out, s + 1)
                for c in range(NC):
                    mm = pe.matmul(bank[:, 0:D], xT[:, t % 2, c, :], w_v[:, c, :], start=(c == 0), stop=(c == NC - 1))
                mm.then_inc(v_proj, 1)

            pe.wait_ge(proj_in, 16 * 6)
            pe.wait_ge(wscaled, 2)
            slice_turn(0, 0, bank_m[0], None)
            slice_turn(1, 1, bank_m[1], None)
            slice_qk(0, 0, bank_m[0])
            for t in range(NT):
                if t + 1 < NT:
                    slice_qk(t + 1, t + 1, bank_m[1 - t % 2])
                slice_v(t, t, bank_m[t % 2])
                if t + 2 < NT:
                    slice_turn(t + 2, t + 2, bank_m[t % 2], None)
            pe.wait_ge(v_out, NT)
            pe.wait_ge(ready, 4)

            def qk(b, u):
                blk, j, q = unit(u)
                g = blk // 2
                pe.wait_ge(summed, b * UNITS + u - 2 + 1 + FREE_S)
                if u % 16 == 0:
                    pe.wait_ge(stacked[g % 2], (b * 2 + g // 2 + 1) * (MOVES * 16))
                mm = pe.matmul(bank_s[u % 2][:, :], stack_q[:, g % 2, j, P * q:P * q + P], stack_k[:, g % 2, j, :],
                               start=True, stop=(j != ON_PE))
                if j == ON_PE:
                    at = b * NT + q
                    mask = mask_add[:, at, :] if isinstance(b, int) else mask_add[:, bass.ds(at, 1), :].rearrange("p o k -> p (o k)")
                    mm = pe.matmul(bank_s[u % 2][:, :], ident_half[:, :], mask, start=False, stop=True)
                mm.then_inc(qk_done, 1)

            def turn(b, u):
                pe.wait_ge(shifted, b * UNITS + u + 1)
                pe.wait_ge(exped, b * UNITS + u - 2 + 1 + FREE_T)
                for k in range(NT):
                    mm = pe.transpose(bank_t[u % 2][:, P * k:P * k + P], scores[:, u % NSC, P * k:P * k + P], ident)
                mm.then_inc(turned, 1)

            def pv(b, blk, k):
                if k == 0:
                    pe.wait_ge(exped, b * UNITS + 8 * blk + 8 + FREE_T)
                    pe.wait_ge(ctx_out, b * HALVES + blk - 2 + 1 + FREE_C)
                    pe.wait_ge(v_moved, b + 1)
                for j in range(4):
                    mm = pe.matmul(bank_c[blk % 2][VW * j:VW * j + VW, 0:HALF], V[:, k, 4 * (blk // 2) + j, :],
                                   probs[:, blk % 2, j, k, :], start=(k == 0), stop=(k == NT - 1))
                if k == NT - 1:
                    mm.then_inc(pv_done, 1)

            def ctx_turn(b, blk):
                pe.wait_ge(ctx_out, b * HALVES + blk + 1 + FREE_C)
                pe.wait_ge(ctx_norm, b * HALVES + blk + FREE_1)
                for q in range(2):
                    mm = pe.transpose(bank_m[0][:, P * q:P * q + P], ctx_raw[:, blk % 2, P * q:P * q + P], ident)
                mm.then_inc(ctx_turned, 1)

            def back_turn(b, i):
                pe.wait_ge(ctx_norm, (b + 1) * HALVES - 1 + i + FREE_1)
                if i == 1:
                    pe.wait_ge(y_done, b * 2 + 1 + FREE_1)
                elif isinstance(b, int) and b == B - 1:
                    pe.wait_ge(v_out, B * NT)
                else:
                    pe.wait_ge(v_out, (b + 2) * NT)
                for c in range(NC):
                    for q in range(2):
                        mm = pe.transpose(bank_m[1][:, P * (2 * c + q):P * (2 * c + q) + P],
                                          ctx_tok[:, 2 * i + q, P * c:P * c + P], ident)
                mm.then_inc(back_turned, 1)

            def project_out(b, i):
                pe.wait_ge(back_out, b * 2 + i + 1)
                for q in range(2):
                    for c in range(NC):
                        at = P * (2 * i + q)
                        mm = pe.matmul(bank_m[1][:, D * q:D * q + D], ctxT[:, c, at:at + P], w_o[:, c, :],
                                       start=(c == 0), stop=(c == NC - 1))
                mm.then_inc(wo_done, 1)

            def batch(b, first, last):
                for u in range(UNITS):
                    blk, p = u // 8, u % 8
                    if u + 2 < UNITS:
                        qk(b, u + 2)
                    elif not last:
                        qk(b + 1, u + 2 - UNITS)
                    if u > 0:
                        turn(b, u - 1)
                    elif not first:
                        turn(b - 1, UNITS - 1)
                    if p == 1:
                        if blk >= 2:
                            ctx_turn(b, blk - 2)
                        elif not first:
                            ctx_turn(b - 1, HALVES - 2 + blk)
                    if 2 <= p < 6:
                        if blk >= 1:
                            pv(b, blk - 1, p - 2)
                        elif not first:
                            pv(b - 1, HALVES - 1, p - 2)
                    for i, at in enumerate(OUT_AT):
                        if u == at and not first:
                            back_turn(b - 1, i)
                        if u == at + 2 and not first:
                            project_out(b - 1, i)
                    if not last:
                        for t, at in enumerate(SLICE_AT):
                            s = (b + 1) * NT + t
                            if u == at:
                                slice_turn(s, t, bank_m[1], b * 2)
                            if u == at + 1:
                                slice_qk(s, t, bank_m[1])
                            if u == at + 3:
                                slice_v(s, t, bank_m[1])

            pe.wait_ge(row_done, 2 * B)
            qk(0, 0)
            qk(0, 1)
            batch(0, True, False)
            with pe.Fori(1, B - 1) as b:
                batch(b, False, False)
            batch(B - 1, False, True)
            turn(B - 1, UNITS - 1)
            ctx_turn(B - 1, HALVES - 2)
            for k in range(NT):
                pv(B - 1, HALVES - 1, k)
            back_turn(B - 1, 0)
            ctx_turn(B - 1, HALVES - 1)
            project_out(B - 1, 0)
            back_turn(B - 1, 1)
            project_out(B - 1, 1)

            def turn_h(b):
                for c in range(NC):
                    for t in range(NT):
                        if c == 0:
                            pe.wait_ge(h_done, b * NT + t + 1)
                        if t == 0:
                            pe.wait_ge(hT_out, b * NC)
                        mm = pe.transpose(bank_s[c][:, P * t:P * t + P], h_now[:, t, P * c:P * c + P], ident)
                    mm.then_inc(h_turned, 1)

            def feed(b, last):
                pe.wait_ge(hT_out, (b + 1) * NC)
                for f in range(NF):
                    pe.wait_ge(gelu_done, b * NF + f - 4 + 1 + FREE_G)
                    for c in range(NC):
                        mm = pe.matmul(ff_bank(f)[:, :], w1_sb[:, c, P * f:P * f + P], hT[:, c, :],
                                       start=(c == 0), stop=(c == NC - 1))
                    mm.then_inc(ff1_done, 1)
                if not last:
                    turn_h(b + 1)
                for t in range(NT):
                    if t >= 2:
                        pe.wait_ge(o_done, b * NT + t - 1 + FREE_1)
                    else:
                        pe.wait_ge(o_done, b * NT + FREE_1)
                    for f in range(NF):
                        if t == 0:
                            pe.wait_ge(gelu_done, b * NF + f + 1 + FREE_G)
                        mm = pe.matmul(bank_m[t % 2][:, 0:D], gT[:, f, P * t:P * t + P], w2_sb[:, f, :],
                                       start=(f == 0), stop=(f == NF - 1))
                    mm.then_inc(ff2_done, 1)

            turn_h(0)
            pe.wait_ge(ffn_in, 32)
            with pe.Fori(0, B - 1) as b:
                feed(b, False)
            feed(B - 1, True)

        @block.vector
        def _(dve):
            for s, n in ((summed, FREE_S), (turned, FREE_SC), (exped, FREE_T), (pv_done, FREE_P), (ctx_out, FREE_C),
                         (ctx_turned, FREE_R), (gelu_done, FREE_G), (ctx_norm, FREE_1), (y_done, FREE_1), (wo_done, FREE_1),
                         (back_turned, FREE_1), (ff2_done, FREE_1), (o_done, FREE_1)):
                dve.sem_inc(s, n)
            steps = [0]

            def step(ins):
                steps[0] += 1
                ins.then_inc(angle_step, 1)
                dve.wait_ge(angle_step, steps[0])

            dve.wait_ge(angles_in, 16 * 6)
            step(dve.tensor_scalar(angle[:, SIN_E:SIN_E + B], t_int[:, :], 0.01, 4000.0, ALU.mult, ALU.mult))
            step(dve.tensor_scalar(angle[:, COS_E:COS_E + B], angle[:, SIN_E:SIN_E + B], cst[:, C_FREQ:C_FREQ + 1], None, ALU.mult))
            step(dve.tensor_copy(angle[:, SIN_E:SIN_E + B], angle[:, COS_E:COS_E + B]))
            step(dve.scalar_tensor_tensor(out=turns[:, :], in0=angle[:, :], scalar=INV_2PI,
                                          in1=cst[:, C_TURN:C_TURN + ANGLES], op0=ALU.mult, op1=ALU.add))
            step(dve.tensor_scalar(turns[:, :], turns[:, :], ROUND, None, ALU.add))
            step(dve.tensor_scalar(turns[:, :], turns[:, :], -ROUND, None, ALU.add))
            for part in (TWO_PI_A, TWO_PI_B, TWO_PI_C):
                in1 = angle[:, :]
                ins = dve.scalar_tensor_tensor(out=angle[:, :], in0=turns[:, :], scalar=-part, in1=in1,
                                               op0=ALU.mult, op1=ALU.add)
                if part != TWO_PI_C:
                    step(ins)
                else:
                    ins.then_inc(minus_done, 1)
                    dve.wait_ge(minus_done, 1)
            dve.tensor_tensor(angle[:, :], angle[:, :], cst[:, C_PHASE:C_PHASE + ANGLES], ALU.add).then_inc(minus_done, 1)
            dve.wait_ge(minus_done, 2)
            step(dve.tensor_scalar(angle[:, :], angle[:, :], -PI_IN, None, ALU.max))
            step(dve.tensor_scalar(angle[:, :], angle[:, :], PI_IN, None, ALU.min))
            dve.wait_ge(sin_done, 1)
            dve.tensor_scalar(minus[:, :], sincos[:, :], -1.0, None, ALU.mult).then_inc(minus_done, 1)
            dve.wait_ge(silu_done, 1)
            dve.tensor_copy(emb_wide, emb[:, :].rearrange("p (c o) -> p c o", o=1).broadcast_to([P, 8, P])).then_inc(wide_done, 1)
            dve.wait_ge(minus_done, 3)
            def sines(b):
                for i, (to, fro, s) in enumerate(((0, 1, sincos[:, SIN_T + b:SIN_T + b + 1]), (1, 0, minus[:, SIN_T + b:SIN_T + b + 1]),
                                                  (2, 3, sincos[:, SIN_P + b:SIN_P + b + 1]), (3, 2, minus[:, SIN_P + b:SIN_P + b + 1]))):
                    if i % 2 == 0:
                        dve.wait_ge(cos_part, 2 * b + i // 2 + 1)
                    src, dst = (v[:, NT * b:NT * b + NT, :].rearrange("p t (n e) -> p (t n) e", e=4) for v in (x_raw, X))
                    dve.scalar_tensor_tensor(out=dst[:, :, to], in0=src[:, :, fro], scalar=s, in1=dst[:, :, to],
                                             op0=ALU.mult, op1=ALU.add).then_inc(rotated, 1)
            def statistics(b):
                dve.wait_ge(rotated, 4 * b + 4)
                for i in range(NT * b, NT * b + NT):
                    dve.bn_stats(stats[:, i, :], X[:, i, :]).then_inc(stat_done, 1)
                for i in range(NT * b, NT * b + NT):
                    dve.wait_ge(stat_done, i + 1)
                    dve.bn_aggr(meanvar[:, i, :], stats[:, i, :]).then_inc(aggr_done, 1)

            sines(0)
            statistics(0)
            for b in range(B):
                src = (bank_s + bank_t)[b]
                dve.wait_ge(emb_done, b + 1)
                if b == 0:
                    dve.wait_ge(ada_in, 32)
                dve.scalar_tensor_tensor(out=row_scale[:, b, 0:D], in0=src[:, 0:D], scalar=1.0, in1=b_ada_row[:, 0:D],
                                         op0=ALU.add, op1=ALU.add).then_inc(row_done, 1)
                dve.tensor_tensor(row_scale[:, b, D:2 * D], src[:, D:2 * D], b_ada_row[:, D:2 * D], ALU.add).then_inc(row_done, 1)
            def reciprocals(lo, hi, n):
                dve.wait_ge(sd_done, n)
                dve.reciprocal(rstd[:, lo:hi], sd[:, lo:hi]).then_inc(rstd_done, 1)
                dve.wait_ge(rstd_done, n)

            reciprocals(0, NT, 1)
            dve.wait_ge(row_done, 2 * B)

            def norm_batch(b):
                for t in range(NT):
                    i = NT * b + t
                    dve.scalar_tensor_tensor(out=X[:, i, :], in0=X[:, i, :], scalar=meanvar[:, i, 0:1],
                                             in1=row_scale[:, b, 0:D], op0=ALU.subtract, op1=ALU.mult).then_inc(centred, 1)
                for t in range(NT):
                    i = NT * b + t
                    dve.wait_ge(centred, i + 1)
                    dve.scalar_tensor_tensor(out=X[:, i, :], in0=X[:, i, :], scalar=rstd[:, i:i + 1],
                                             in1=row_scale[:, b, D:2 * D], op0=ALU.mult, op1=ALU.add).then_inc(normed, 1)

            def qk_bias(s, bank):
                dve.wait_ge(qk_proj, s + 1)
                dve.wait_ge(rest1, s)
                dve.wait_ge(cast1, s)
                dve.tensor_tensor(qk_full[:, :, :], bank[:, :].rearrange("p (m n) -> p m n", m=4),
                                  b_qk[:, :].rearrange("p (m o) -> p m o", o=1).broadcast_to([P, 4, P]), ALU.add)\
                    .then_inc(qk_out, 1)

            def v_bias(s, t, b, bank):
                dve.wait_ge(v_proj, s + 1)
                if t == 0:
                    dve.wait_ge(v_moved, b)
                dve.tensor_tensor(V_next[:, t, :, 0:DH], bank[:, 0:D].rearrange("p (h w) -> p h w", h=H),
                                  bv_row[:, :].rearrange("p (h w) -> p h w", h=H), ALU.add).then_inc(v_out, 1)

            norm_batch(0)
            dve.wait_ge(wscaled, 2)
            dve.wait_ge(rows_in, 16 * 6)
            dve.wait_ge(ready, 3)
            qk_bias(0, bank_m[0])
            for t in range(NT):
                if t + 1 < NT:
                    qk_bias(t + 1, bank_m[1 - t % 2])
                v_bias(t, t, 0, bank_m[t % 2])
            for b in range(1, B):
                sines(b)
                statistics(b)
            reciprocals(NT, TILES, 2)
            for b in range(1, B):
                norm_batch(b)

            def await_sum(b, u):
                dve.wait_ge(qk_done, b * UNITS + u + 1)
                blk, j, q = unit(u)
                if j != ON_PE:
                    dve.wait_ge(masked, b * POOL_MASKS + 3 * blk + j + 1)
                dve.wait_ge(turned, b * UNITS + u - NSC + 1 + FREE_SC)

            def sum_max(b, u):
                c = u // 4
                dve.tensor_tensor_reduce(out=scores[:, u % NSC, :], in0=bank_s[u % 2][:, :],
                                         in1=ring[:, c % RING, u % 4 // 2, u % 2, :], scale=1.0, scalar=LOWEST,
                                         op0=ALU.add, op1=ALU.max, accum_out=row_max[:, u % NSC:u % NSC + 1]).then_inc(summed, 1)

            def shift(b, u, last=False):
                dve.wait_ge(summed, b * UNITS + u + 1 + FREE_S)
                if u + 2 < UNITS:
                    await_sum(b, u + 2)
                elif not last:
                    await_sum(b + 1, u + 2 - UNITS)
                dve.tensor_scalar(scores[:, u % NSC, :], scores[:, u % NSC, :], row_max[:, u % NSC:u % NSC + 1], None,
                                  ALU.subtract).then_inc(shifted, 1)

            def denominator(b, blk):
                dve.wait_ge(ctx_turned, b * HALVES + blk + 1 + FREE_R)
                dve.reciprocal(ctx_sum[:, :, :], bank_m[0][:, 0:HALF].rearrange("p (q h w) -> p q h w", q=2, h=4)[:, :, :, ONE])\
                    .then_inc(ctx_recip, 1)

            def divide(b, blk):
                dve.wait_ge(ctx_recip, b * HALVES + blk + 1)
                if blk == 0:
                    dve.wait_ge(back_turned, b * 2 + FREE_1)
                q0, g = 2 * (blk % 2), blk // 2
                for q in range(2):
                    src = bank_m[0][:, P * q:P * q + P].rearrange("p (h w) -> p h w", h=4)[:, :, 0:DH]
                    ins = dve.tensor_tensor(ctx_tok[:, q0 + q, 4 * DH * g:4 * DH * (g + 1)].rearrange("p (h w) -> p h w", h=4),
                                            src, ctx_sum[:, q, :].rearrange("p (h o) -> p h o", o=1).broadcast_to([P, 4, DH]),
                                            ALU.mult)
                ins.then_inc(ctx_norm, 1)

            def residual(b, i):
                src = bank_m[1][:, :].rearrange("p (q d) -> p q d", q=2)
                dst = X[:, bass.ds(b * NT + 2 * i, 2), :]
                dve.wait_ge(wo_done, b * 2 + i + 1 + FREE_1)
                dve.tensor_tensor(dst, src, dst, ALU.add).then_inc(wo_bias, 1)
                dve.wait_ge(wo_bias, b * 2 + i + 1)
                dve.tensor_tensor(dst, dst, bo_row[:, :].rearrange("p (o d) -> p o d", o=1).broadcast_to([P, 2, D]), ALU.add)\
                    .then_inc(y_done, 1)

            def residual_stats(b, i):
                dve.wait_ge(y_done, b * 2 + i + 1 + FREE_1)
                for q in range(2):
                    at = b * NT + 2 * i + q
                    dve.bn_stats(stats2[:, bass.ds(at, 1), :].rearrange("p o s -> p (o s)"),
                                 X[:, bass.ds(at, 1), :].rearrange("p o s -> p (o s)")).then_inc(stat_done, 1)

            def batch(b, first, last):
                for u in range(UNITS):
                    blk, p = u // 8, u % 8
                    if first and u < 2:
                        await_sum(b, u)
                    sum_max(b, u)
                    if u > 0:
                        shift(b, u - 1, last)
                    elif not first:
                        shift(b - 1, UNITS - 1)
                    if u == 7:
                        dve.wait_ge(v_out, (b + 1) * NT)
                        dve.wait_ge(pv_done, b * HALVES + FREE_P)
                        dve.tensor_copy(V[:, :, :, :], V_next[:, :, :, :]).then_inc(v_moved, 1)
                    if p in (3, 4) and (blk >= 2 or not first):
                        what = denominator if p == 3 else divide
                        if blk >= 2:
                            what(b, blk - 2)
                        else:
                            what(b - 1, HALVES - 2 + blk)
                    for i, at in enumerate(OUT_AT):
                        if u == at + 3 and not first:
                            residual(b - 1, i)
                        if u == at + 4 and not first:
                            residual_stats(b - 1, i)
                    if not last:
                        for t, at in enumerate(SLICE_AT):
                            s = (b + 1) * NT + t
                            if u == at + 2:
                                qk_bias(s, bank_m[1])
                            if u == at + 4:
                                v_bias(s, t, b + 1, bank_m[1])

            batch(0, True, False)
            with dve.Fori(1, B - 1) as b:
                batch(b, False, False)
            batch(B - 1, False, True)
            shift(B - 1, UNITS - 1, True)
            for blk in (HALVES - 2, HALVES - 1):
                denominator(B - 1, blk)
                divide(B - 1, blk)
            for i in range(2):
                residual(B - 1, i)
            for i in range(2):
                residual_stats(B - 1, i)

            for i in range(TILES):
                dve.wait_ge(stat_done, TILES + i + 1)
                dve.bn_aggr(meanvar2[:, i, :], stats2[:, i, :]).then_inc(aggr_done, 1)
            dve.wait_ge(sd_done, 3)
            dve.reciprocal(rstd2[:, :], sd2[:, :]).then_inc(rstd_done, 1)
            dve.wait_ge(rstd_done, 3)

            def normalise(b):
                dve.wait_ge(h_turned, b * NC)
                for t in range(NT):
                    at = b * NT + t
                    dve.tensor_scalar(h_now[:, t, :], X[:, bass.ds(at, 1), :].rearrange("p o d -> p (o d)"),
                                      meanvar2[:, bass.ds(at, 1), 0], rstd2[:, bass.ds(at, 1)],
                                      ALU.subtract, ALU.mult).then_inc(h_done, 1)

            def finish(b):
                dve.wait_ge(yb_done, b + 1)
                for t in range(NT):
                    dve.wait_ge(ff2_done, b * NT + t + 1 + FREE_1)
                    dve.tensor_tensor(o_sb[:, b % 2, t, :], bank_m[t % 2][:, 0:D], yb[:, t, :], ALU.add).then_inc(o_done, 1)

            normalise(0)
            for b in range(B):
                if b + 1 < B:
                    normalise(b + 1)
                if b >= 2:
                    dve.wait_ge(out_in[b % 2], 16 * NT * (b // 2))
                finish(b)



_INS = ["x", "condB_theta", "condB_phi", "itok_B_34_63", "fside_Bx16xSxS_0", "mask_Bx1xSxS_bk0",
        "L1_cond_W_ada", "L1_cond_b_ada", "L1_cond_Wq", "L1_cond_bq", "L1_cond_Wk", "L1_cond_bk",
        "L1_cond_Wv", "L1_cond_bv", "L1_cond_Wo", "L1_cond_bo", "L1_cond_W1", "L1_cond_b1",
        "L1_cond_W2", "L1_cond_b2", "L1_cond_g2", "L1_cond_beta2"]

_COLUMNS = ["bq", "bk", "b1", "g2", "beta2"]


def kernel(**inputs):
    import concourse.bacc as bacc
    from concourse.bass_utils import run_bass_kernel_spmd as run

    nc = bacc.Bacc("TRN2", target_bir_lowering=False, num_devices=1)
    arrays, args = {}, []
    for name in _INS + ["constants"]:
        a = np.ascontiguousarray(constants() if name == "constants" else inputs[name])
        if a.dtype == np.bool_:
            a = a.view(np.uint32)
        if name.removeprefix("L1_cond_") in _COLUMNS:
            a = np.ascontiguousarray(a.reshape(-1, P).T)
        arrays[f"in_{name}"] = a
        args.append(nc.dram_tensor(f"in_{name}", a.shape, mybir.dt.from_np(a.dtype), kind="ExternalInput").ap())
    out = nc.dram_tensor("out", (B, S, D), F32, kind="ExternalOutput").ap()
    rotate_then_attend_then_feed_forward(nc, *args, out)
    r = run(nc, [arrays], core_ids=[0])
    return r.results[0]["out"]
```

```python
from contextlib import ExitStack
import math

import numpy as np

import concourse.bass as bass
from concourse import mybir

F32 = mybir.dt.float32
F32R = mybir.dt.float32r
BF16 = mybir.dt.bfloat16
I32 = mybir.dt.int32
U8 = mybir.dt.uint8
U32 = mybir.dt.uint32
ALU = mybir.AluOpType
ACT = mybir.ActivationFunctionType

B, S, D, H, DH, F = 4, 512, 256, 16, 16, 1024
P = 128
NT = S // P
TILES = B * NT
NC = D // P
NF = F // P
QUADS = H // 4
HALF = 2 * P
HALVES = 2 * QUADS
UNITS = 8 * HALVES
LOADS = UNITS // 4
RING = 4
NSB = 4
NSC = 8
LEAD = 3
VW = 32
ONE = DH

EPS = 1e-5
MASKED = -1e30
LOWEST = -3.0e38
INV_2PI = 1.0 / (2.0 * math.pi)
ROUND = 12582912.0
TWO_PI_A = 6.28125
TWO_PI_B = float(np.float32(np.round((2.0 * math.pi - TWO_PI_A) * 2**22) / 2**22))
TWO_PI_C = 2.0 * math.pi - TWO_PI_A - TWO_PI_B
PI_IN = 3.1415925

TERMS = [(0, 1), (0, 0), (0, 2), (1, 0), (1, 1), (2, 0)]
ROWS = len(TERMS) * DH
PAIRS = [(0, 0), (0, 1), (1, 0)]
MOVES = 2

STORES = []
for side in range(2):
    for part in range(3):
        at = [i for i, term in enumerate(TERMS) if term[side] == part]
        step = at[1] - at[0] if len(at) > 1 else 1
        assert at == list(range(at[0], at[-1] + 1, step))
        STORES.append((side, part, at[0], at[-1], step))

SIN_E, COS_E, COS_T, SIN_T, COS_P, SIN_P, ANGLES = 0, 4, 8, 12, 16, 20, 24
C_ID, C_FREQ, C_TURN, C_PHASE, C_ALL = 0, P, P + 1, P + 1 + 24, P + 1 + 48

SLICE_AT = [12, 23, 29, 35]
OUT_AT = [7, 18]
PV_AT, COPY_AT, CTX_TURN_AT, DENOM_AT, DIVIDE_AT = 6, 8, 11, 14, 14
V_COPY_AT = 9
QK_BIAS_AT, CAST_AT, SLICE_V_AT, V_BIAS_AT, RESIDUAL_AT = 4, 3, 4, 6, 5
NORM_AT = [4, 7, 18, 21, 26, 30, 34, 38, 42, 46, 50, 54]
CAST2_AT, REST_AT, REST2_AT = 6, 13, 17
STORE_AT, STACK_AT = [47, 62], 53
ON_PE = 3
POOL_MASKS = 3 * HALVES


def constants():
    c = np.zeros((P, C_ALL), np.float32)
    c[:, C_ID:C_ID + P] = np.eye(P, dtype=np.float32)
    step = np.float32(-math.log(10000.0) / (P - 1))
    c[:, C_FREQ] = np.exp(np.arange(P, dtype=np.float32) * step)
    for at in (COS_E, COS_T, COS_P):
        c[:, C_TURN + at:C_TURN + at + 4] = 0.25
        c[:, C_PHASE + at:C_PHASE + at + 4] = math.pi / 2
    return c


def rotate_then_attend_then_feed_forward(nc, x, theta, phi, timestep, bias, mask, w_ada, b_ada, wq, bq, wk, bk,
                                         wv, bv, wo, bo, w1, b1, w2, b2, g2, beta2, const, out):
    with ExitStack() as ctx:
        def sb(name, shape, dt=F32, stack=ctx):
            return stack.enter_context(nc.sbuf_tensor(name, shape, dt))

        def sem(name):
            return ctx.enter_context(nc.semaphore(name))

        term_rows = nc.dram_tensor("term_rows", (4, P, len(TERMS), S), BF16, kind="Internal").ap()

        bank_s = [ctx.enter_context(nc.psum_tensor(f"bank_s{i}", [P, S], F32)) for i in range(NSB)]
        bank_t = [ctx.enter_context(nc.psum_tensor(f"bank_t{i}", [P, S], F32)) for i in range(2)]
        bank_c = ctx.enter_context(nc.psum_tensor("bank_c", [P, S], F32))
        bank_m = ctx.enter_context(nc.psum_tensor("bank_m", [P, S], F32))
        pair = [bank_c, bank_m]
        bank_of = [bank_c, bank_m] + bank_t
        bank_ctx = bank_c[:, 0:HALF]
        bank_ctx_t = bank_c[:, HALF:2 * HALF]

        qk_full = sb("qk_full", [P, 2, 4, P])
        qk_rest = sb("qk_rest", [P, 2, 4, P])
        x_now = sb("x_now", [P, 2, D])
        xT = sb("xT", [P, 2, NC, P])
        X = sb("X", [P, TILES, D])
        ctx_raw = sb("ctx_raw", [P, 2, HALF])
        ctx_sum = sb("ctx_sum", [P, 2, 4])
        ctx_tok = sb("ctx_tok", [P, NT, D])
        ctxT = sb("ctxT", [P, NC, S])
        cst = sb("cst", [P, C_ALL])
        w_qk = sb("w_qk", [P, NC, 2 * D])
        w_v = sb("w_v", [P, NC, D])
        w_o = sb("w_o", [P, NC, D])
        b_qk = sb("b_qk", [P, 4])
        bv_row = sb("bv_row", [P, D])
        bo_row = sb("bo_row", [P, D])
        b2_row = sb("b2_row", [P, D])
        b1_col = sb("b1_col", [P, NF])
        g2_col = sb("g2_col", [P, NC])
        beta2_col = sb("beta2_col", [P, NC])
        eps = sb("eps", [P, 1])
        pool_spare = sb("pool_spare", [P, 2 * RING])
        dve_spare = sb("dve_spare", [P, 2])
        t_int = sb("t_int", [P, B], I32)
        angle = sb("angle", [P, ANGLES])
        turns = sb("turns", [P, ANGLES])
        sincos = sb("sincos", [P, ANGLES])
        minus = sb("minus", [P, ANGLES])
        emb = sb("emb", [P, 8])
        stats = sb("stats", [P, TILES, 6])
        meanvar = sb("meanvar", [P, TILES, 2])
        stats2 = sb("stats2", [P, TILES, 6])
        meanvar2 = sb("meanvar2", [P, TILES, 2])
        sd = sb("sd", [P, TILES])
        rstd = sb("rstd", [P, TILES])
        sd2 = sb("sd2", [P, TILES])
        rstd2 = sb("rstd2", [P, TILES])
        ident_half = sb("ident_half", [P, P], BF16)
        row_scale = sb("row_scale", [P, B, 2 * D])
        row_max = sb("row_max", [P, NSC])
        attention = ExitStack()
        ring = sb("ring", [P, RING, 2, 2, S], stack=attention)
        probs = sb("probs", [P, 2, 4, NT, HALF], stack=attention)
        parts = sb("parts", [P, 3, 4, S], BF16, stack=attention)
        mask_add = sb("mask_add", [P, TILES, S], BF16, stack=attention)
        scores = sb("scores", [P, NSC, S], stack=attention)
        stack_q = sb("stack_q", [ROWS, 2, 4, S], BF16, stack=attention)
        stack_k = sb("stack_k", [ROWS, 2, 4, S], BF16, stack=attention)
        V = sb("V", [P, NT, H, VW], stack=attention)
        V_next = sb("V_next", [P, NT, H, DH], stack=attention)
        attention.close()

        w1_parts = sb("w1_parts", [P, 2, NC, F], F32R)
        w2_parts = sb("w2_parts", [P, 2, NF, D], F32R)
        gT_parts = sb("gT_parts", [P, 2, NF, S], F32R)
        w1_raw = sb("w1_raw", [P, NC, F])
        yT = sb("yT", [P, NC, S])
        w2_raw = sb("w2_raw", [P, NF, D])
        hT_parts = sb("hT_parts", [P, 2, NC, S], F32R)
        g_now = sb("g_now", [P, 4, S])
        yb = sb("yb", [P, NT, D])
        hT = sb("hT", [P, NC, S])
        h_now = sb("h_now", [P, NT, D])
        o_sb = sb("o_sb", [P, 2, 2, D])

        ident = cst[:, C_ID:C_ID + P]

        flat = probs[:, :, :, :, :].rearrange("p a h k q -> p (a h k q)")
        x_raw = flat[:, 0:TILES * D].rearrange("p (t d) -> p t d", t=TILES)
        mask_words = flat[:, TILES * D:TILES * D + TILES * S // 4].bitcast(U32)
        mask_raw = mask_words.bitcast(U8).rearrange("p (t k) -> p t k", t=TILES)
        emb_wide = ctx_tok[:, :, :].rearrange("p t d -> p (t d)").rearrange("p (c n) -> p c n", c=2 * B)
        w_ada_sb = ctxT[:, :, :]
        b_ada_row = ctx_raw[:, :, :].rearrange("p a n -> p (a n)")
        angles_in = sem("angles_in")
        x_in = [sem(f"x_in{b}") for b in range(B)]
        mask_in = [sem(f"mask_in{i}") for i in range(2)]
        ada_in = sem("ada_in")
        proj_in = sem("proj_in")
        rows_in = sem("rows_in")
        w1_in = sem("w1_in")
        w2_in = sem("w2_in")
        bias_in = [[sem(f"bias_in{i}_{h}") for h in range(2)] for i in range(RING)]
        stored = sem("stored")
        stacked = [sem(f"stacked{i}") for i in range(2)]
        out_in = [sem(f"out_in{i}") for i in range(2)]
        ready = sem("ready")
        angle_step = sem("angle_step")
        sin_done = sem("sin_done")
        silu_done = sem("silu_done")
        wide_done = sem("wide_done")
        emb_done = sem("emb_done")
        row_done = sem("row_done")
        minus_done = sem("minus_done")
        cos_part = sem("cos_part")
        rotated = sem("rotated")
        stat_done = sem("stat_done")
        aggr_done = sem("aggr_done")
        sd_done = sem("sd_done")
        rstd_done = sem("rstd_done")
        centred = sem("centred")
        normed = sem("normed")
        mask_done = sem("mask_done")
        wscaled = sem("wscaled")
        x_copied = sem("x_copied")
        x_turned = sem("x_turned")
        xT_out = sem("xT_out")
        qk_proj = sem("qk_proj")
        qk_out = sem("qk_out")
        v_proj = sem("v_proj")
        v_out = sem("v_out")
        cast1 = sem("cast1")
        rest1 = sem("rest1")
        cast2 = sem("cast2")
        rest2 = sem("rest2")
        v_moved = sem("v_moved")
        masked = sem("masked")
        qk_done = sem("qk_done")
        summed = sem("summed")
        shifted = sem("shifted")
        shifted_act = sem("shifted_act")
        turned = sem("turned")
        exped = sem("exped")
        pv_done = sem("pv_done")
        ctx_out = sem("ctx_out")
        ctx_turned = sem("ctx_turned")
        ctx_recip = sem("ctx_recip")
        ctx_norm = sem("ctx_norm")
        back_turned = sem("back_turned")
        back_out = sem("back_out")
        wo_done = sem("wo_done")
        wo_bias = sem("wo_bias")
        y_done = sem("y_done")
        h_done = sem("h_done")
        h_turned = sem("h_turned")
        hT_out = sem("hT_out")
        hT_high = sem("hT_high")
        hT_split = sem("hT_split")
        w1_high = sem("w1_high")
        w1_split = sem("w1_split")
        w2_high = sem("w2_high")
        w2_split = sem("w2_split")
        ff1_done = sem("ff1_done")
        gelu_done = sem("gelu_done")
        g_high = sem("g_high")
        g_split = sem("g_split")
        ff2_done = sem("ff2_done")
        yT_out = sem("yT_out")
        y_turned = sem("y_turned")
        yb_done = sem("yb_done")
        o_done = sem("o_done")

        FREE_S, FREE_SC, FREE_T, FREE_P, FREE_C, FREE_R, FREE_1 = NSB, NSC, 2, 2, 1, 2, 1

        def unit(u):
            blk, j, q = u // 8, u % 8 // 2, u % 2
            return blk, j, 2 * (blk % 2) + q

        def block_at(u, after):
            return (u - after) // 8 - 1 if (u - after) % 8 == 0 else None

        def left_over(after):
            return [of for of in range(HALVES) if 8 * (of + 1) + after >= UNITS]

        def by_act(u):
            return u % 4 == 3

        def ff_bank(f):
            return (bank_t + bank_s[2:4])[f % 4]

        block = ctx.enter_context(nc.Block())

        def await_all(eng, *pairs):
            pairs = [(s, n if isinstance(n, int) else eng.snap(n)) for s, n in pairs]
            for s, n in pairs:
                eng.wait_ge(s, n)

        def stack(eng, b, g, first=False):
            through = [] if first else [(qk_done, b * UNITS + 16 * (g - 1))]
            in_dram = [(stored, 16 * len(STORES) if first else b * (32 * len(STORES)) + (16 if g == 0 else 32) * len(STORES))]
            await_all(eng, *through, *in_dram)
            r = 64 * (g % 2)
            for dst, m in ((stack_q, g // 2), (stack_k, 2 + g // 2)):
                eng.dma_start(dst[:, g % 2, :, :], term_rows[m, r:r + 64].rearrange("(h d) s n -> (d s) h n", h=4))\
                    .then_inc(stacked[g % 2], 16)

        def stored_before(b):
            return b * (32 * len(STORES))

        def store_parts(eng, b, i):
            if i == 0:
                eng.wait_ge(rest2, NT * (b + 1))
                eng.wait_ge(cast2, NT * (b + 1))
                if not isinstance(b, int) or b > 0:
                    for j in range(2):
                        eng.wait_ge(stacked[j], b * (2 * MOVES * 16))
            for side, part, lo, hi, step in STORES:
                m = 2 * side + i
                n = (hi - lo) // step + 1
                eng.dma_start(term_rows[m, :, lo:hi + 1:step, :],
                              parts[:, part, m:m + 1, :].broadcast_to([P, n, S])).then_inc(stored, 16)

        def first_rest(eng, s, t):
            eng.wait_ge(qk_out, s + 1)
            eng.wait_ge(cast1, s + 1)
            if not isinstance(s, int) or s > 1:
                eng.wait_ge(cast2, s - 1)
                eng.wait_ge(rest2, s - 1)
            eng.tensor_tensor(qk_rest[:, t % 2, :, :], qk_full[:, t % 2, :, :], parts[:, 0, :, P * t:P * t + P], ALU.subtract)\
                .then_inc(rest1, 1)

        def second_rest(eng, s, t):
            eng.wait_ge(rest1, s + 1)
            eng.wait_ge(cast2, s + 1)
            eng.tensor_tensor(parts[:, 2, :, P * t:P * t + P], qk_rest[:, t % 2, :, :], parts[:, 1, :, P * t:P * t + P],
                              ALU.subtract).then_inc(rest2, 1)

        @block.sync
        def _(sp):
            sp.dma_start(cst[:, :], const).then_inc(angles_in, 16)
            sp.dma_start(t_int[:, :], timestep.rearrange("(o b) -> o b", o=1).broadcast_to([P, B])).then_inc(angles_in, 16)
            for src, at in ((theta, COS_T), (phi, COS_P)):
                sp.dma_start(angle[:, at:at + 2 * B].rearrange("p (r b) -> p r b", r=2),
                             src.rearrange("(o r b) -> o r b", o=1, r=1).broadcast_to([P, 2, B])).then_inc(angles_in, 16)
            sp.dma_start(x_raw[:, 0:NT, :], x[0].rearrange("(t p) d -> p t d", p=P)).then_inc(x_in[0], 16)
            sp.dma_start(w_ada_sb, w_ada.rearrange("(c p) n -> p c n", p=P)).then_inc(ada_in, 16)
            sp.dma_start(b_ada_row, b_ada.rearrange("(o n) -> o n", o=1).broadcast_to([P, 2 * D])).then_inc(ada_in, 16)
            for w, at in ((wq, 0), (wk, D)):
                sp.dma_start(w_qk[:, :, at:at + D], w.rearrange("(c p) n -> p c n", p=P)).then_inc(proj_in, 16)
            for v, at in ((bq, 0), (bk, 2)):
                sp.dma_start(b_qk[:, at:at + 2], v).then_inc(proj_in, 16)
            sp.dma_start(w_v[:, :, :], wv.rearrange("(c p) n -> p c n", p=P)).then_inc(proj_in, 16)
            sp.dma_start(bv_row[:, :], bv.rearrange("(o n) -> o n", o=1).broadcast_to([P, D])).then_inc(proj_in, 16)

            def load_mask(lo, hi, i):
                sp.dma_start(mask_words.rearrange("p (t k) -> p t k", t=TILES)[:, NT * lo:NT * hi, :],
                             mask[lo:hi].rearrange("b o (t p) k -> p (b o t) k", p=P)).then_inc(mask_in[i], 16)

            load_mask(0, 1, 0)

            def load_bias(b, c, first=False):
                blk, h = c // 2, 4 * (c // 4) + 2 * (c % 2)
                q0 = HALF * (blk % 2)
                src = bias[b] if first else bias[bass.ds(b, 1)].rearrange("o h q k -> (o h) q k")
                for i in range(2):
                    if not first:
                        sp.wait_ge(summed, b * UNITS + 4 * (c - RING) + 2 * i + 2 + FREE_S)
                    sp.dma_start(ring[:, c % RING, i, :, :], src[h + i, q0:q0 + HALF, :].rearrange("(t p) k -> p t k", p=P))\
                        .then_inc(bias_in[c % RING][i], 16)

            for c in range(2):
                load_bias(0, c, first=True)
            for b in range(1, B):
                sp.dma_start(x_raw[:, NT * b:NT * b + NT, :], x[b].rearrange("(t p) d -> p t d", p=P)).then_inc(x_in[b], 16)
            load_mask(1, B, 1)
            store_parts(sp, 0, 0)
            stack(sp, 0, 0, first=True)
            stack(sp, 0, 1, first=True)
            for c in range(2, RING):
                load_bias(0, c, first=True)
            store_parts(sp, 0, 1)
            sp.dma_start(w_o[:, :, :], wo.rearrange("(c p) n -> p c n", p=P)).then_inc(rows_in, 16)
            for v, row in ((bo, bo_row), (b2, b2_row)):
                sp.dma_start(row[:, :], v.rearrange("(o n) -> o n", o=1).broadcast_to([P, D])).then_inc(rows_in, 16)
            sp.dma_start(b1_col[:, :], b1).then_inc(rows_in, 16)
            sp.dma_start(g2_col[:, :], g2).then_inc(rows_in, 16)
            sp.dma_start(beta2_col[:, :], beta2).then_inc(rows_in, 16)
            sp.wait_ge(stored, stored_before(1))

            def batch(b, last):
                for c in range(RING, LOADS + RING):
                    if c < LOADS:
                        load_bias(b, c)
                    elif not last:
                        load_bias(b + 1, c - LOADS)
                    if c == 6:
                        stack(sp, b, 2)
                    if c == 10:
                        stack(sp, b, 3)
                if not last:
                    stack(sp, b + 1, 1)

            with sp.Fori(0, B - 1) as b:
                batch(b, False)
            batch(B - 1, True)

            sp.wait_ge(stored, stored_before(B))
            sp.dma_start(w1_raw[:, :, :], w1.rearrange("(c p) f -> p c f", p=P)).then_inc(w1_in, 16)
            sp.wait_ge(qk_done, B * UNITS)
            sp.dma_start(w2_raw[:, :, :], w2.rearrange("(c p) d -> p c d", p=P)).then_inc(w2_in, 16)
            with sp.Fori(0, B) as b:
                for i in range(2):
                    sp.wait_ge(o_done, b * 2 + i + 1)
                    dst = out[bass.ds(b, 1), HALF * i:HALF * i + HALF, :].rearrange("o (q p) d -> p (o q) d", p=P)
                    sp.dma_start(dst, o_sb[:, i, :, :]).then_inc(out_in[i], 16)
            for i in range(2):
                sp.wait_ge(out_in[i], 16 * B)

        @block.gpsimd
        def _(pool):
            pool.memset(eps[:, :], EPS).then_inc(ready, 1)
            pool.memset(V[:, :, :, :], 0.0).then_inc(ready, 1)
            pool.wait_ge(ready, 2)
            pool.memset(V[:, :, :, ONE:ONE + 1], 1.0).then_inc(ready, 1)
            pool.wait_ge(angles_in, 16 * 4)
            pool.tensor_copy(ident_half[:, :], ident).then_inc(ready, 1)

            def mask_bias(b, c, h):
                pool.wait_ge(bias_in[c % RING][h], (b * (LOADS // RING) + c // RING + 1) * 16)
                pool.tensor_tensor(pool_spare[:, 2 * (c % RING) + h:2 * (c % RING) + h + 1], eps[:, :], eps[:, :], ALU.add)
                q = 2 * (c // 2 % 2)
                src = ring[:, c % RING, h, :, :]
                pool.tensor_tensor(src, src, mask_add[:, bass.ds(b * NT + q, 2), :], ALU.add).then_inc(masked, 1)

            def mask_load(b, c):
                for h in range(2):
                    if 2 * (c % 2) + h != ON_PE:
                        mask_bias(b, c, h)

            pool.wait_ge(mask_done, 1)
            for c in range(2):
                mask_load(0, c)
            def batch(b, last):
                for c in range(2, LOADS + 2):
                    if c < LOADS:
                        mask_load(b, c)
                    elif not last:
                        pool.wait_ge(mask_done, 2)
                        mask_load(b + 1, c - LOADS)
                    for t, at in enumerate(SLICE_AT):
                        if not last:
                            if c == (at + REST_AT) // 4:
                                first_rest(pool, (b + 1) * NT + t, t)
                            if c == (at + REST2_AT) // 4:
                                second_rest(pool, (b + 1) * NT + t, t)

            with pool.Fori(0, B - 1) as b:
                batch(b, False)
            batch(B - 1, True)

            pool.wait_ge(w2_high, 1)
            pool.tensor_tensor(w2_parts[:, 1, :, :], w2_raw[:, :, :], w2_parts[:, 0, :, :], ALU.subtract).then_inc(w2_split, 1)
            pool.wait_ge(rows_in, 16 * 6)

            def add_b2(b, first=False):
                if first:
                    pool.wait_ge(y_done, B * 2 + FREE_1)
                    pool.wait_ge(turned, B * UNITS + FREE_SC)
                else:
                    pool.wait_ge(o_done, b * 2)
                pool.tensor_tensor(yb[:, :, :], X[:, bass.ds(b * NT, NT), :],
                                   b2_row[:, :].rearrange("p (o d) -> p o d", o=1).broadcast_to([P, NT, D]),
                                   ALU.add).then_inc(yb_done, 1)

            add_b2(0, first=True)
            with pool.Fori(1, B) as b:
                add_b2(b)

        @block.scalar
        def _(act):
            act.wait_ge(angle_step, 10)
            act.activation(sincos[:, :], angle[:, :], ACT.Sin).then_inc(sin_done, 1)
            act.wait_ge(sin_done, 1)
            act.activation(emb[:, :], sincos[:, SIN_E:COS_E + B], ACT.Silu).then_inc(silu_done, 1)
            def cosines(b):
                act.wait_ge(x_in[b], 16)
                for pair, at in ((0, COS_T), (2, COS_P)):
                    src, dst = (v[:, NT * b:NT * b + NT, :].rearrange("p t (n e) -> p (t n) e", e=4)[:, :, pair:pair + 2]
                                for v in (x_raw, X))
                    act.activation(dst, src, ACT.Copy, scale=sincos[:, at + b:at + b + 1]).then_inc(cos_part, 1)
            def deviations(lo, hi):
                act.wait_ge(aggr_done, hi)
                act.activation(sd[:, lo:hi], meanvar[:, lo:hi, 1], ACT.Sqrt, bias=eps[:, 0:1]).then_inc(sd_done, 1)

            def masks(lo, hi):
                act.activation(mask_add[:, lo:hi, :], mask_raw[:, lo:hi, :], ACT.Copy, scale=MASKED).then_inc(mask_done, 1)

            cosines(0)
            act.wait_ge(ready, 1)
            deviations(0, NT)
            act.wait_ge(proj_in, 16 * 6)
            act.activation(w_qk[:, :, 0:D], w_qk[:, :, 0:D], ACT.Copy, scale=DH ** -0.5).then_inc(wscaled, 1)
            act.activation(b_qk[:, 0:2], b_qk[:, 0:2], ACT.Copy, scale=DH ** -0.5).then_inc(wscaled, 1)

            def copy_x(s, t):
                if not isinstance(s, int) or s > 1:
                    act.wait_ge(x_turned, s - 1)
                src = X[:, bass.ds(s, 1), :].rearrange("p o d -> p (o d)")
                act.activation(x_now[:, t % 2, :], src, ACT.Copy).then_inc(x_copied, 1)

            def copy_xT(s, t, bank):
                act.wait_ge(x_turned, s + 1)
                if not isinstance(s, int) or s > 1:
                    act.wait_ge(v_proj, s - 1)
                act.activation(xT[:, t % 2, :, :], bank[:, 0:NC * P].rearrange("p (c n) -> p c n", c=NC), ACT.Copy)\
                    .then_inc(xT_out, 1)

            def cast_first(s, t, b, first=False):
                act.wait_ge(qk_out, s + 1)
                if t == 0 and not first:
                    act.wait_ge(stored, stored_before(b))
                act.activation(parts[:, 0, :, P * t:P * t + P], qk_full[:, t % 2, :, :], ACT.Copy).then_inc(cast1, 1)

            def cast_second(s, t):
                act.wait_ge(rest1, s + 1)
                act.activation(parts[:, 1, :, P * t:P * t + P], qk_rest[:, t % 2, :, :], ACT.Copy).then_inc(cast2, 1)

            for t in range(2):
                copy_xT(t, t, bank_of[t])
            for t in range(NT):
                cast_first(t, t, 0, first=True)
                if t + 2 < NT:
                    copy_xT(t + 2, t + 2, bank_of[t + 2])
                cast_second(t, t)
                if t + 1 < B:
                    cosines(t + 1)
            act.wait_ge(mask_in[0], 16)
            masks(0, NT)
            act.wait_ge(mask_in[1], 16)
            masks(NT, TILES)
            deviations(NT, TILES)

            def shift_act(b, u):
                act.wait_ge(summed, b * UNITS + u + 1 + FREE_S)
                act.activation(scores[:, u % NSC, :], scores[:, u % NSC, :], ACT.Identity, scale=-1.0,
                               bias=row_max[:, u % NSC:u % NSC + 1]).then_inc(shifted_act, 1)

            def exp(b, u):
                blk, j, q = unit(u)
                if u % 8 == 0:
                    act.wait_ge(pv_done, b * HALVES + blk - 2 + 1 + FREE_P)
                act.wait_ge(turned, b * UNITS + u + 1 + FREE_SC)
                act.activation(probs[:, blk % 2, j, :, P * (q % 2):P * (q % 2) + P],
                               bank_t[u % 2][:, :].rearrange("p (k q) -> p k q", k=NT), ACT.Exp,
                               scale=-1.0 if by_act(u) else 1.0).then_inc(exped, 1)

            def copy_ctx(b, blk):
                act.wait_ge(pv_done, b * HALVES + blk + 1 + FREE_P)
                act.wait_ge(ctx_turned, b * HALVES + blk - 2 + 1 + FREE_R)
                act.activation(ctx_raw[:, blk % 2, :], bank_ctx, ACT.Copy).then_inc(ctx_out, 1)

            def copy_back(b, i):
                act.wait_ge(back_turned, b * 2 + i + 1 + FREE_1)
                act.wait_ge(wo_done, b * 2 + FREE_1)
                act.activation(ctxT[:, :, HALF * i:HALF * i + HALF],
                               bank_m[:, :].rearrange("p (c n) -> p c n", c=NC), ACT.Copy).then_inc(back_out, 1)

            def batch(b, first, last):
                for u in range(UNITS):
                    if u + 2 < UNITS and by_act(u + 2):
                        shift_act(b, u + 2)
                    exp(b, u)
                    of = block_at(u, COPY_AT)
                    if of is not None and of >= 0:
                        copy_ctx(b, of)
                    elif of is not None and not first:
                        copy_ctx(b - 1, HALVES + of)
                    if u == V_COPY_AT:
                        act.wait_ge(v_out, (b + 1) * NT)
                        act.wait_ge(ready, 3)
                        act.wait_ge(pv_done, b * HALVES + FREE_P)
                        act.activation(V[:, :, :, 0:DH], V_next[:, :, :, :], ACT.Copy).then_inc(v_moved, 1)
                    if not first and u in (OUT_AT[0], OUT_AT[1]):
                        copy_back(b - 1, OUT_AT.index(u))
                    if not last and u in STORE_AT:
                        store_parts(act, b + 1, STORE_AT.index(u))
                    if not last and u == STACK_AT:
                        stack(act, b + 1, 0)
                    if not last:
                        for t, at in enumerate(SLICE_AT):
                            s = (b + 1) * NT + t
                            if u == at - 3:
                                if first:
                                    act.wait_ge(normed, s + 1)
                                copy_x(s, t)
                            if u == at - 1:
                                copy_xT(s, t, bank_m)
                            if u == at + CAST_AT:
                                cast_first(s, t, b + 1)
                            if u == at + CAST2_AT:
                                cast_second(s, t)

            batch(0, True, False)
            act.wait_ge(normed, TILES)
            with act.Fori(1, B - 1) as b:
                batch(b, False, False)
            batch(B - 1, False, True)

            def deviations2(lo, hi):
                act.wait_ge(aggr_done, TILES + hi)
                act.activation(sd2[:, lo:hi], meanvar2[:, lo:hi, 1], ACT.Sqrt, bias=eps[:, 0:1]).then_inc(sd_done, 1)

            def copy_hT(b, first=False):
                for c in range(NC):
                    act.wait_ge(h_turned, b * NC + c + 1)
                    if not first:
                        act.wait_ge(hT_split, b * NC)
                    act.activation(hT[:, c, :], bank_s[c][:, :], ACT.Identity, scale=g2_col[:, c:c + 1],
                                   bias=beta2_col[:, c:c + 1]).then_inc(hT_out, 1)

            def high(b, f):
                act.wait_ge(gelu_done, b * NF + f + 1)
                act.activation(gT_parts[:, 0, f, :], g_now[:, f % 4, :], ACT.Copy).then_inc(g_high, 1)

            def feed(b, first=False, last=False):
                for f in range(NF):
                    act.wait_ge(ff1_done, b * NF + f + 1)
                    if not first or f >= 4:
                        act.wait_ge(g_split, b * NF + f - 4 + 1)
                    if not first and f == 0:
                        act.wait_ge(ff2_done, b * NC)
                    act.activation(g_now[:, f % 4, :], ff_bank(f)[:, :], ACT.Gelu_apprx_sigmoid, bias=b1_col[:, f:f + 1])\
                        .then_inc(gelu_done, 1)
                    if f > 0:
                        high(b, f - 1)
                high(b, NF - 1)
                if not last:
                    copy_hT(b + 1)

            for of in left_over(COPY_AT):
                copy_ctx(B - 1, of)
                if of == HALVES - 2:
                    deviations2(0, TILES - NT)
            act.wait_ge(rows_in, 16 * 6)
            copy_hT(0, first=True)
            copy_back(B - 1, 0)
            copy_back(B - 1, 1)
            act.wait_ge(w2_in, 16)
            act.activation(w2_parts[:, 0, :, :], w2_raw[:, :, :], ACT.Copy).then_inc(w2_high, 1)
            deviations2(TILES - NT, TILES)
            feed(0, first=True)
            with act.Fori(1, B - 1) as b:
                feed(b)
            feed(B - 1, last=True)

        @block.tensor
        def _(pe):
            pe.wait_ge(wide_done, 1)
            pe.wait_ge(ada_in, 32)
            def embed(b):
                for c in range(NC):
                    mm = pe.matmul(bank_s[b][:, :], emb_wide[:, c * B + b, :], w_ada_sb[:, c, :],
                                   start=(c == 0), stop=(c == NC - 1))
                mm.then_inc(emb_done, 1)

            embed(0)

            def slice_turn(s, t, bank, y_before):
                pe.wait_ge(x_copied, s + 1 - NT)
                pe.wait_ge(v_out, s)
                outs = sum(at < SLICE_AT[t] for at in OUT_AT)
                if isinstance(y_before, int):
                    outs = 2
                pe.wait_ge(y_done, y_before - 2 + outs + FREE_1)
                for c in range(NC):
                    mm = pe.transpose(bank[:, P * c:P * c + P], x_now[:, t % 2, P * c:P * c + P], ident)
                mm.then_inc(x_turned, 1)

            def slice_qk(s, t, bank):
                pe.wait_ge(xT_out, s + 1)
                for m in range(4):
                    for c in range(NC):
                        mm = pe.matmul(bank[:, P * m:P * m + P], w_qk[:, c, P * m:P * m + P], xT[:, t % 2, c, :],
                                       start=(c == 0), stop=(c == NC - 1))
                mm.then_inc(qk_proj, 1)

            def slice_v(s, t, bank):
                pe.wait_ge(qk_out, s + 1)
                for c in range(NC):
                    mm = pe.matmul(bank[:, 0:D], xT[:, t % 2, c, :], w_v[:, c, :], start=(c == 0), stop=(c == NC - 1))
                mm.then_inc(v_proj, 1)

            for t in range(NT):
                pe.wait_ge(normed, t + 1)
                for c in range(NC):
                    mm = pe.transpose(bank_of[t][:, P * c:P * c + P], X[:, t, P * c:P * c + P], ident)
                mm.then_inc(x_turned, 1)
            pe.wait_ge(proj_in, 16 * 6)
            pe.wait_ge(wscaled, 2)
            slice_qk(0, 0, bank_of[0])
            for t in range(NT):
                if t + 1 < NT:
                    slice_qk(t + 1, t + 1, bank_of[t + 1])
                slice_v(t, t, bank_of[t])
            for b in range(1, B):
                embed(b)
            pe.wait_ge(v_out, NT)
            pe.wait_ge(ready, 4)

            def qk(b, u):
                blk, j, q = unit(u)
                g = blk // 2
                pe.wait_ge(summed, b * UNITS + u - NSB + 1 + FREE_S)
                if u % 16 == 0:
                    pe.wait_ge(stacked[g % 2], (b * 2 + g // 2 + 1) * (MOVES * 16))
                mm = pe.matmul(bank_s[u % NSB][:, :], stack_q[:, g % 2, j, P * q:P * q + P], stack_k[:, g % 2, j, :],
                               start=True, stop=(j != ON_PE))
                if j == ON_PE:
                    at = b * NT + q
                    mask = mask_add[:, at, :] if isinstance(b, int) else mask_add[:, bass.ds(at, 1), :].rearrange("p o k -> p (o k)")
                    mm = pe.matmul(bank_s[u % NSB][:, :], ident_half[:, :], mask, start=False, stop=True)
                mm.then_inc(qk_done, 1)

            def turn(b, u):
                if by_act(u):
                    pe.wait_ge(shifted_act, b * (UNITS // 4) + u // 4 + 1)
                else:
                    pe.wait_ge(shifted, b * (UNITS - UNITS // 4) + u + 1 - (u + 1) // 4)
                pe.wait_ge(exped, b * UNITS + u - 2 + 1 + FREE_T)
                for k in range(NT):
                    mm = pe.transpose(bank_t[u % 2][:, P * k:P * k + P], scores[:, u % NSC, P * k:P * k + P], ident)
                mm.then_inc(turned, 1)

            def pv(b, blk, k):
                if k == 0:
                    pe.wait_ge(exped, b * UNITS + 8 * blk + 8 + FREE_T)
                    pe.wait_ge(ctx_norm, b * HALVES + blk + FREE_1)
                    pe.wait_ge(v_moved, b + 1)
                for j in range(4):
                    mm = pe.matmul(bank_ctx[VW * j:VW * j + VW, :], V[:, k, 4 * (blk // 2) + j, :],
                                   probs[:, blk % 2, j, k, :], start=(k == 0), stop=(k == NT - 1))
                if k == NT - 1:
                    mm.then_inc(pv_done, 1)

            def ctx_turn(b, blk):
                pe.wait_ge(ctx_out, b * HALVES + blk + 1 + FREE_C)
                for q in range(2):
                    mm = pe.transpose(bank_ctx_t[:, P * q:P * q + P], ctx_raw[:, blk % 2, P * q:P * q + P], ident)
                mm.then_inc(ctx_turned, 1)

            def back_turn(b, i):
                pe.wait_ge(ctx_norm, (b + 1) * HALVES - 1 + i + FREE_1)
                if i == 1:
                    pe.wait_ge(y_done, b * 2 + 1 + FREE_1)
                if isinstance(b, int) and b >= B - 2:
                    pe.wait_ge(v_out, B * NT)
                else:
                    pe.wait_ge(v_out, (b + 2) * NT + sum(at < OUT_AT[i] for at in SLICE_AT))
                for c in range(NC):
                    for q in range(2):
                        mm = pe.transpose(bank_m[:, P * (2 * c + q):P * (2 * c + q) + P],
                                          ctx_tok[:, 2 * i + q, P * c:P * c + P], ident)
                mm.then_inc(back_turned, 1)

            def project_out(b, i):
                pe.wait_ge(back_out, b * 2 + i + 1)
                for q in range(2):
                    for c in range(NC):
                        at = P * (2 * i + q)
                        mm = pe.matmul(bank_m[:, D * q:D * q + D], ctxT[:, c, at:at + P], w_o[:, c, :],
                                       start=(c == 0), stop=(c == NC - 1))
                mm.then_inc(wo_done, 1)

            def batch(b, first, last):
                for u in range(UNITS):
                    blk, p = u // 8, u % 8
                    if u + LEAD < UNITS:
                        qk(b, u + LEAD)
                    elif not last:
                        qk(b + 1, u + LEAD - UNITS)
                    if u > 0:
                        turn(b, u - 1)
                    elif not first:
                        turn(b - 1, UNITS - 1)
                    of = block_at(u, CTX_TURN_AT)
                    if of is not None and of >= 0:
                        ctx_turn(b, of)
                    elif of is not None and not first:
                        ctx_turn(b - 1, HALVES + of)
                    for k in range(NT):
                        of = block_at(u, PV_AT + k)
                        if of is not None and of >= 0:
                            pv(b, of, k)
                        elif of is not None and not first:
                            pv(b - 1, HALVES + of, k)
                    for i, at in enumerate(OUT_AT):
                        if u == at and not first:
                            back_turn(b - 1, i)
                        if u == at + 2 and not first:
                            project_out(b - 1, i)
                    if not last:
                        for t, at in enumerate(SLICE_AT):
                            s = (b + 1) * NT + t
                            if u == at:
                                slice_turn(s, t, bank_m, b * 2)
                            if u == at + 1:
                                slice_qk(s, t, bank_m)
                            if u == at + SLICE_V_AT:
                                slice_v(s, t, bank_m)

            pe.wait_ge(row_done, 2 * B)
            for u in range(LEAD):
                qk(0, u)
            batch(0, True, False)
            pe.wait_ge(rows_in, 16 * 6)
            with pe.Fori(1, B - 1) as b:
                batch(b, False, False)
            batch(B - 1, False, True)
            turn(B - 1, UNITS - 1)
            def turn_h(b, first=False):
                for c in range(NC):
                    for t in range(NT):
                        if c == 0:
                            pe.wait_ge(h_done, b * NT + t + 1)
                        if c == 0 and t == 0 and not first:
                            pe.wait_ge(hT_out, b * NC)
                        mm = pe.transpose(bank_s[c][:, P * t:P * t + P], h_now[:, t, P * c:P * c + P], ident)
                    mm.then_inc(h_turned, 1)

            def back_y(b):
                pe.wait_ge(yT_out, b * NC + NC)
                pe.wait_ge(hT_out, b * NC + NC)
                for i in range(2):
                    for q in range(2):
                        for c in range(NC):
                            mm = pe.transpose(bank_s[i][:, D * q + P * c:D * q + P * c + P],
                                              yT[:, c, P * (2 * i + q):P * (2 * i + q) + P], ident)
                    mm.then_inc(y_turned, 1)

            def feed(b, first=False, last=False):
                pe.wait_ge(hT_split, b * NC + NC)
                for f in range(NF):
                    if not first or f >= 4:
                        pe.wait_ge(gelu_done, b * NF + f - 4 + 1)
                    for c in range(NC):
                        for n, (i, j) in enumerate(PAIRS):
                            mm = pe.matmul(ff_bank(f)[:, :], w1_parts[:, i, c, P * f:P * f + P], hT_parts[:, j, c, :],
                                           start=(c == 0 and n == 0), stop=(c == NC - 1 and n == len(PAIRS) - 1))
                    mm.then_inc(ff1_done, 1)
                    if f == 1 and not first:
                        back_y(b - 1)
                if not last:
                    if not first:
                        pe.wait_ge(o_done, b * 2)
                    turn_h(b + 1)
                if first:
                    pe.wait_ge(w2_split, 1)
                for m in range(NC):
                    if not first:
                        pe.wait_ge(yT_out, (b - 1) * NC + m + 1)
                    elif m == 1:
                        pe.wait_ge(y_done, B * 2 + FREE_1)
                    for f in range(NF):
                        if m == 0:
                            pe.wait_ge(g_split, b * NF + f + 1)
                        for n, (i, j) in enumerate(PAIRS):
                            mm = pe.matmul(pair[m][:, :], w2_parts[:, i, f, P * m:P * m + P], gT_parts[:, j, f, :],
                                           start=(f == 0 and n == 0), stop=(f == NF - 1 and n == len(PAIRS) - 1))
                    mm.then_inc(ff2_done, 1)

            for u in range(UNITS, UNITS + CTX_TURN_AT + 1):
                for what, at in [(ctx_turn, CTX_TURN_AT)] + [(pv, PV_AT + k) for k in range(NT)]:
                    of = block_at(u, at)
                    if of is not None and of < HALVES:
                        what(B - 1, of, *([at - PV_AT] if what is pv else []))
                if u == UNITS + PV_AT + NT - 1:
                    turn_h(0, first=True)
            back_turn(B - 1, 0)
            project_out(B - 1, 0)
            back_turn(B - 1, 1)
            project_out(B - 1, 1)
            pe.wait_ge(w1_split, 1)
            feed(0, first=True)
            with pe.Fori(1, B - 1) as b:
                feed(b)
            feed(B - 1, last=True)
            back_y(B - 1)

        @block.vector
        def _(dve):
            for s, n in ((summed, FREE_S), (turned, FREE_SC), (exped, FREE_T), (pv_done, FREE_P), (ctx_out, FREE_C),
                         (ctx_turned, FREE_R), (ctx_norm, FREE_1), (y_done, FREE_1), (wo_done, FREE_1),
                         (back_turned, FREE_1)):
                dve.sem_inc(s, n)
            steps = [0]

            def step(ins):
                steps[0] += 1
                ins.then_inc(angle_step, 1)
                dve.wait_ge(angle_step, steps[0])

            dve.wait_ge(angles_in, 16 * 4)
            step(dve.tensor_scalar(angle[:, SIN_E:SIN_E + B], t_int[:, :], 0.01, 4000.0, ALU.mult, ALU.mult))
            step(dve.tensor_scalar(angle[:, COS_E:COS_E + B], angle[:, SIN_E:SIN_E + B], cst[:, C_FREQ:C_FREQ + 1], None, ALU.mult))
            step(dve.tensor_copy(angle[:, SIN_E:SIN_E + B], angle[:, COS_E:COS_E + B]))
            step(dve.scalar_tensor_tensor(out=turns[:, :], in0=angle[:, :], scalar=INV_2PI,
                                          in1=cst[:, C_TURN:C_TURN + ANGLES], op0=ALU.mult, op1=ALU.add))
            step(dve.tensor_scalar(turns[:, :], turns[:, :], ROUND, None, ALU.add))
            step(dve.tensor_scalar(turns[:, :], turns[:, :], -ROUND, None, ALU.add))
            for part in (TWO_PI_A, TWO_PI_B, TWO_PI_C):
                in1 = angle[:, :]
                ins = dve.scalar_tensor_tensor(out=angle[:, :], in0=turns[:, :], scalar=-part, in1=in1,
                                               op0=ALU.mult, op1=ALU.add)
                if part != TWO_PI_C:
                    step(ins)
                else:
                    ins.then_inc(minus_done, 1)
                    dve.wait_ge(minus_done, 1)
            dve.tensor_tensor(angle[:, :], angle[:, :], cst[:, C_PHASE:C_PHASE + ANGLES], ALU.add).then_inc(minus_done, 1)
            dve.wait_ge(minus_done, 2)
            step(dve.tensor_scalar(angle[:, :], angle[:, :], -PI_IN, None, ALU.max))
            step(dve.tensor_scalar(angle[:, :], angle[:, :], PI_IN, None, ALU.min))
            dve.wait_ge(sin_done, 1)
            dve.tensor_scalar(minus[:, :], sincos[:, :], -1.0, None, ALU.mult).then_inc(minus_done, 1)
            dve.wait_ge(silu_done, 1)
            dve.tensor_copy(emb_wide, emb[:, :].rearrange("p (c o) -> p c o", o=1).broadcast_to([P, 8, P])).then_inc(wide_done, 1)
            dve.wait_ge(minus_done, 3)
            def sines(b):
                for i, (to, fro, s) in enumerate(((0, 1, sincos[:, SIN_T + b:SIN_T + b + 1]), (1, 0, minus[:, SIN_T + b:SIN_T + b + 1]),
                                                  (2, 3, sincos[:, SIN_P + b:SIN_P + b + 1]), (3, 2, minus[:, SIN_P + b:SIN_P + b + 1]))):
                    if i % 2 == 0:
                        dve.wait_ge(cos_part, 2 * b + i // 2 + 1)
                    src, dst = (v[:, NT * b:NT * b + NT, :].rearrange("p t (n e) -> p (t n) e", e=4) for v in (x_raw, X))
                    dve.scalar_tensor_tensor(out=dst[:, :, to], in0=src[:, :, fro], scalar=s, in1=dst[:, :, to],
                                             op0=ALU.mult, op1=ALU.add).then_inc(rotated, 1)
            def statistics(b):
                dve.wait_ge(rotated, 4 * b + 4)
                for i in range(NT * b, NT * b + NT):
                    dve.bn_stats(stats[:, i, :], X[:, i, :]).then_inc(stat_done, 1)
                for i in range(NT * b, NT * b + NT):
                    dve.wait_ge(stat_done, i + 1)
                    dve.bn_aggr(meanvar[:, i, :], stats[:, i, :]).then_inc(aggr_done, 1)

            sines(0)
            statistics(0)
            def row_scales(b):
                src = bank_s[b]
                dve.wait_ge(emb_done, b + 1)
                if b == 0:
                    dve.wait_ge(ada_in, 32)
                dve.scalar_tensor_tensor(out=row_scale[:, b, 0:D], in0=src[:, 0:D], scalar=1.0, in1=b_ada_row[:, 0:D],
                                         op0=ALU.add, op1=ALU.add).then_inc(row_done, 1)
                dve.tensor_tensor(row_scale[:, b, D:2 * D], src[:, D:2 * D], b_ada_row[:, D:2 * D], ALU.add).then_inc(row_done, 1)

            def reciprocals(lo, hi, n):
                dve.wait_ge(sd_done, n)
                dve.reciprocal(rstd[:, lo:hi], sd[:, lo:hi]).then_inc(rstd_done, 1)
                dve.wait_ge(rstd_done, n)

            def centre(i):
                dve.wait_ge(row_done, 2 * (i // NT) + 2)
                dve.scalar_tensor_tensor(out=X[:, i, :], in0=X[:, i, :], scalar=meanvar[:, i, 0:1],
                                         in1=row_scale[:, i // NT, 0:D], op0=ALU.subtract, op1=ALU.mult).then_inc(centred, 1)

            def norm(i):
                dve.wait_ge(centred, i + 1)
                dve.scalar_tensor_tensor(out=X[:, i, :], in0=X[:, i, :], scalar=rstd[:, i:i + 1],
                                         in1=row_scale[:, i // NT, D:2 * D], op0=ALU.mult, op1=ALU.add).then_inc(normed, 1)

            row_scales(0)
            reciprocals(0, NT, 1)

            def qk_bias(s, t, bank):
                dve.wait_ge(qk_proj, s + 1)
                if not isinstance(s, int) or s > 1:
                    dve.wait_ge(rest1, s - 1)
                    dve.wait_ge(cast1, s - 1)
                dve.tensor_tensor(qk_full[:, t % 2, :, :], bank[:, :].rearrange("p (m n) -> p m n", m=4),
                                  b_qk[:, :].rearrange("p (m o) -> p m o", o=1).broadcast_to([P, 4, P]), ALU.add)\
                    .then_inc(qk_out, 1)

            def v_bias(s, t, b, bank):
                dve.wait_ge(v_proj, s + 1)
                if t == 0:
                    dve.wait_ge(v_moved, b)
                dve.tensor_tensor(V_next[:, t, :, :], bank[:, 0:D].rearrange("p (h w) -> p h w", h=H),
                                  bv_row[:, :].rearrange("p (h w) -> p h w", h=H), ALU.add).then_inc(v_out, 1)

            centre(0)
            for t in range(NT):
                if t + 1 < NT:
                    centre(t + 1)
                norm(t)
            dve.wait_ge(wscaled, 2)
            dve.wait_ge(proj_in, 16 * 6)
            dve.wait_ge(ready, 3)
            qk_bias(0, 0, bank_of[0])
            for t in range(NT):
                first_rest(dve, t, t)
                if t + 1 < NT:
                    qk_bias(t + 1, t + 1, bank_of[t + 1])
                second_rest(dve, t, t)
                v_bias(t, t, 0, bank_of[t])
            for b in range(1, B):
                sines(b)
                statistics(b)
                row_scales(b)
            reciprocals(NT, TILES, 2)

            def await_sum(b, u):
                dve.wait_ge(qk_done, b * UNITS + u + 1)
                blk, j, q = unit(u)
                if j != ON_PE:
                    dve.wait_ge(masked, b * POOL_MASKS + 3 * blk + j + 1)
                elif q % 2 == 0:
                    c = u // 4
                    dve.wait_ge(bias_in[c % RING][1], (b * (LOADS // RING) + c // RING + 1) * 16)
                dve.wait_ge(turned, b * UNITS + u - NSC + 1 + FREE_SC)

            def sum_max(b, u):
                c = u // 4
                dve.tensor_tensor_reduce(out=scores[:, u % NSC, :], in0=bank_s[u % NSB][:, :],
                                         in1=ring[:, c % RING, u % 4 // 2, u % 2, :], scale=1.0, scalar=LOWEST,
                                         op0=ALU.add, op1=ALU.max, accum_out=row_max[:, u % NSC:u % NSC + 1]).then_inc(summed, 1)

            def shift(b, u, last=False):
                if not by_act(u):
                    dve.wait_ge(summed, b * UNITS + u + 1 + FREE_S)
                if u + 2 < UNITS:
                    await_sum(b, u + 2)
                elif not last:
                    await_sum(b + 1, u + 2 - UNITS)
                if by_act(u):
                    dve.tensor_copy(dve_spare[:, 0:1], eps[:, :])
                else:
                    dve.tensor_scalar(scores[:, u % NSC, :], scores[:, u % NSC, :], row_max[:, u % NSC:u % NSC + 1], None,
                                      ALU.subtract).then_inc(shifted, 1)

            def denominator(b, blk):
                dve.wait_ge(ctx_turned, b * HALVES + blk + 1 + FREE_R)
                dve.reciprocal(ctx_sum[:, :, :], bank_ctx_t.rearrange("p (q h w) -> p q h w", q=2, h=4)[:, :, :, ONE])\
                    .then_inc(ctx_recip, 1)

            def divide(b, blk):
                dve.wait_ge(ctx_recip, b * HALVES + blk + 1)
                if blk == 0:
                    dve.wait_ge(back_turned, b * 2 + FREE_1)
                q0, g = 2 * (blk % 2), blk // 2
                for q in range(2):
                    src = bank_ctx_t[:, P * q:P * q + P].rearrange("p (h w) -> p h w", h=4)[:, :, 0:DH]
                    ins = dve.tensor_tensor(ctx_tok[:, q0 + q, 4 * DH * g:4 * DH * (g + 1)].rearrange("p (h w) -> p h w", h=4),
                                            src, ctx_sum[:, q, :].rearrange("p (h o) -> p h o", o=1).broadcast_to([P, 4, DH]),
                                            ALU.mult)
                ins.then_inc(ctx_norm, 1)

            def residual(b, i):
                src = bank_m[:, :].rearrange("p (q d) -> p q d", q=2)
                dst = X[:, bass.ds(b * NT + 2 * i, 2), :]
                dve.wait_ge(wo_done, b * 2 + i + 1 + FREE_1)
                dve.tensor_tensor(dst, src, dst, ALU.add).then_inc(wo_bias, 1)
                dve.wait_ge(wo_bias, b * 2 + i + 1)
                dve.tensor_tensor(dst, dst, bo_row[:, :].rearrange("p (o d) -> p o d", o=1).broadcast_to([P, 2, D]), ALU.add)\
                    .then_inc(y_done, 1)

            def residual_stats(b, i):
                dve.wait_ge(y_done, b * 2 + i + 1 + FREE_1)
                for q in range(2):
                    at = b * NT + 2 * i + q
                    dve.bn_stats(stats2[:, bass.ds(at, 1), :].rearrange("p o s -> p (o s)"),
                                 X[:, bass.ds(at, 1), :].rearrange("p o s -> p (o s)")).then_inc(stat_done, 1)

            def batch(b, first, last):
                for u in range(UNITS):
                    blk, p = u // 8, u % 8
                    if first and u < 2:
                        await_sum(b, u)
                    sum_max(b, u)
                    if u > 0:
                        shift(b, u - 1, last)
                    elif not first:
                        shift(b - 1, UNITS - 1)
                    for what, at in ((denominator, DENOM_AT), (divide, DIVIDE_AT)):
                        of = block_at(u, at)
                        if of is not None and of >= 0:
                            what(b, of)
                        elif of is not None and not first:
                            what(b - 1, HALVES + of)
                    for i, at in enumerate(OUT_AT):
                        if u == at + RESIDUAL_AT and not first:
                            residual(b - 1, i)
                        if u == at + RESIDUAL_AT + 1 and not first:
                            residual_stats(b - 1, i)
                    if first and u in NORM_AT:
                        i = NT + NORM_AT.index(u)
                        centre(i)
                        norm(i)
                    if not last:
                        for t, at in enumerate(SLICE_AT):
                            s = (b + 1) * NT + t
                            if u == at + QK_BIAS_AT:
                                qk_bias(s, t, bank_m)
                            if u == at + V_BIAS_AT:
                                v_bias(s, t, b + 1, bank_m)

            batch(0, True, False)
            dve.wait_ge(normed, TILES)
            dve.wait_ge(rows_in, 16 * 6)
            with dve.Fori(1, B - 1) as b:
                batch(b, False, False)
            batch(B - 1, False, True)
            shift(B - 1, UNITS - 1, True)
            def normalise(b, first=False):
                if first:
                    dve.wait_ge(v_moved, B)
                else:
                    dve.wait_ge(h_turned, b * NC)
                for t in range(NT):
                    at = b * NT + t
                    dve.tensor_scalar(h_now[:, t, :], X[:, bass.ds(at, 1), :].rearrange("p o d -> p (o d)"),
                                      meanvar2[:, bass.ds(at, 1), 0], rstd2[:, bass.ds(at, 1)],
                                      ALU.subtract, ALU.mult).then_inc(h_done, 1)

            def split_hT(b, first=False):
                for c in range(NC):
                    dve.wait_ge(hT_out, b * NC + c + 1)
                    if not first:
                        dve.wait_ge(ff1_done, b * NF)
                    dve.tensor_copy(hT_parts[:, 0, c, :], hT[:, c, :]).then_inc(hT_high, 1)
                for c in range(NC):
                    dve.wait_ge(hT_high, b * NC + c + 1)
                    dve.tensor_tensor(hT_parts[:, 1, c, :], hT[:, c, :], hT_parts[:, 0, c, :], ALU.subtract).then_inc(hT_split, 1)

            def finish(b, first=False):
                dve.wait_ge(yb_done, b + 1)
                for i in range(2):
                    dve.wait_ge(y_turned, b * 2 + i + 1)
                    if not first:
                        dve.wait_ge(out_in[i], b * 16)
                    dve.tensor_tensor(o_sb[:, i, :, :], bank_s[i][:, :].rearrange("p (q d) -> p q d", q=2),
                                      yb[:, 2 * i:2 * i + 2, :], ALU.add).then_inc(o_done, 1)

            def feed(b, first=False, last=False):
                for f in range(NF):
                    dve.wait_ge(g_high, b * NF + f + 1)
                    dve.tensor_tensor(gT_parts[:, 1, f, :], g_now[:, f % 4, :], gT_parts[:, 0, f, :], ALU.subtract)\
                        .then_inc(g_split, 1)
                    if f == 2 and not first:
                        finish(b - 1, first=isinstance(b, int) and b == 1)
                    if f == 3 and not last:
                        normalise(b + 1)
                if not last:
                    split_hT(b + 1)
                for m in range(NC):
                    dve.wait_ge(ff2_done, b * NC + m + 1)
                    if not first:
                        dve.wait_ge(y_turned, b * 2)
                    dve.tensor_copy(yT[:, m, :], pair[m][:, :]).then_inc(yT_out, 1)

            def aggregate(lo, hi):
                for i in range(lo, hi):
                    dve.wait_ge(stat_done, TILES + i + 1)
                    dve.bn_aggr(meanvar2[:, i, :], stats2[:, i, :]).then_inc(aggr_done, 1)

            def reciprocals2(lo, hi, n):
                dve.wait_ge(sd_done, n)
                dve.reciprocal(rstd2[:, lo:hi], sd2[:, lo:hi]).then_inc(rstd_done, 1)
                dve.wait_ge(rstd_done, n)

            aggregate(0, TILES - NT)
            dve.wait_ge(w1_in, 16)
            dve.tensor_copy(w1_parts[:, 0, :, :], w1_raw[:, :, :]).then_inc(w1_high, 1)
            denominator(B - 1, HALVES - 2)
            divide(B - 1, HALVES - 2)
            reciprocals2(0, TILES - NT, 3)
            normalise(0, first=True)
            dve.wait_ge(w1_high, 1)
            dve.tensor_tensor(w1_parts[:, 1, :, :], w1_raw[:, :, :], w1_parts[:, 0, :, :], ALU.subtract).then_inc(w1_split, 1)
            denominator(B - 1, HALVES - 1)
            divide(B - 1, HALVES - 1)
            split_hT(0, first=True)
            for i in range(2):
                residual(B - 1, i)
            for i in range(2):
                residual_stats(B - 1, i)
            aggregate(TILES - NT, TILES)
            reciprocals2(TILES - NT, TILES, 4)
            feed(0, first=True)
            feed(1)
            with dve.Fori(2, B - 1) as b:
                feed(b)
            feed(B - 1, last=True)
            finish(B - 1)


_INS = ["x", "condB_theta", "condB_phi", "itok_B_34_63", "fside_Bx16xSxS_0", "mask_Bx1xSxS_bk0",
        "L1_cond_W_ada", "L1_cond_b_ada", "L1_cond_Wq", "L1_cond_bq", "L1_cond_Wk", "L1_cond_bk",
        "L1_cond_Wv", "L1_cond_bv", "L1_cond_Wo", "L1_cond_bo", "L1_cond_W1", "L1_cond_b1",
        "L1_cond_W2", "L1_cond_b2", "L1_cond_g2", "L1_cond_beta2"]

_COLUMNS = ["bq", "bk", "b1", "g2", "beta2"]


def kernel(**inputs):
    import concourse.bacc as bacc
    from concourse.bass_utils import run_bass_kernel_spmd as run

    nc = bacc.Bacc("TRN2", target_bir_lowering=False, num_devices=1)
    arrays, args = {}, []
    for name in _INS + ["constants"]:
        a = np.ascontiguousarray(constants() if name == "constants" else inputs[name])
        if a.dtype == np.bool_:
            a = a.view(np.uint32)
        if name.removeprefix("L1_cond_") in _COLUMNS:
            a = np.ascontiguousarray(a.reshape(-1, P).T)
        arrays[f"in_{name}"] = a
        args.append(nc.dram_tensor(f"in_{name}", a.shape, mybir.dt.from_np(a.dtype), kind="ExternalInput").ap())
    out = nc.dram_tensor("out", (B, S, D), F32, kind="ExternalOutput").ap()
    rotate_then_attend_then_feed_forward(nc, *args, out)
    r = run(nc, [arrays], core_ids=[0])
    return r.results[0]["out"]
```
